# Optimizing a Trainium2 kernel written in Bass

```python
import numpy as np
import jax
import jax.numpy as jnp

def _softmax(x, axis=-1):
    return jax.nn.softmax(x, axis=axis)

def _gelu(x):
    return jax.nn.gelu(x, approximate=True)

def _silu(x):
    return jax.nn.silu(x)

def _sigmoid(x):
    return jax.nn.sigmoid(x)

def _layernorm(x, axis=-1, eps=1e-05):
    m = jnp.mean(x, axis=axis, keepdims=True)
    v = jnp.var(x, axis=axis, keepdims=True)
    return (x - m) / jnp.sqrt(v + eps)

def _scatter_add(tgt, idx, src, axis=0):
    return tgt.at[idx].add(src)

def _segment_sum(src, seg, n):
    return jax.ops.segment_sum(src, seg, n)
kernel_name = 'mk_early_fusion_d2_tok_img256_r4_397de2'

def setup_inputs(seed: int=0):
    np.random.seed(seed)
    _w = jnp.asarray

    def _rec_inputs():
        import jax
        import jax.numpy as jnp
        _rk = jax.random.key(seed)
        x = 7.22013e-05 + 1.00017 * jax.random.normal(jax.random.fold_in(_rk, 1), (2, 64, 64, 64), jnp.float32)
        txt = 0.00220843 + 2.0805 * jax.random.normal(jax.random.fold_in(_rk, 2), (2, 128, 64), jnp.float32)
        return (x, txt)
    x, txt = _rec_inputs()

    def _L0_tok_setup():
        import jax, jax.numpy as jnp
        import numpy as np
        K = 3
        PAD = (K - 1) // 2
        BN_EPS = 1e-05

        def _unfold(x):
            b, c, h, w = x.shape
            xp = jnp.pad(x, ((0, 0), (0, 0), (PAD, PAD), (PAD, PAD)))
            shifts = [xp[:, :, i:i + h, j:j + w] for i in range(K) for j in range(K)]
            return jnp.stack(shifts, axis=2)
        key = jax.random.key(seed)
        ks = jax.random.split(key, 4)
        b, c, h, w = (8, 64, 64, 64)
        cr = c // 4
        x = jax.random.normal(ks[0], (b, c, h, w), dtype=jnp.float32)
        conv1_w = jax.random.normal(ks[1], (cr, c), dtype=jnp.float32) * (1.0 / np.sqrt(c))
        conv1_b = jnp.zeros((cr,), dtype=jnp.float32)
        bn_gamma = jnp.ones((cr,), dtype=jnp.float32)
        bn_beta = jnp.zeros((cr,), dtype=jnp.float32)
        bn_mean = jnp.zeros((cr,), dtype=jnp.float32)
        bn_var = jnp.ones((cr,), dtype=jnp.float32)
        conv2_w = jax.random.normal(ks[2], (K * K, cr), dtype=jnp.float32) * (1.0 / np.sqrt(cr))
        conv2_b = jnp.zeros((K * K,), dtype=jnp.float32)
        return {'x': x, 'conv1_w': conv1_w, 'conv1_b': conv1_b, 'bn_gamma': bn_gamma, 'bn_beta': bn_beta, 'bn_mean': bn_mean, 'bn_var': bn_var, 'conv2_w': conv2_w, 'conv2_b': conv2_b}
    _L0_tok_all = _L0_tok_setup()
    _L0_tok_in = {k: v for k, v in _L0_tok_all.items() if k in ('conv1_w', 'conv1_b', 'bn_gamma', 'bn_beta', 'bn_mean', 'bn_var', 'conv2_w', 'conv2_b')}
    del _L0_tok_all

    def _L0_attn_setup():
        import jax, jax.numpy as jnp
        import numpy as np
        DIM = 64
        HEADS = 4
        HEAD_DIM = DIM // HEADS
        SCALE = HEAD_DIM ** (-0.5)
        key = jax.random.key(seed)
        ks = jax.random.split(key, 9)
        B, N, C = (2, 1024, DIM)
        x = jax.random.normal(ks[0], (B, N, C), dtype=jnp.float32)
        lim = np.sqrt(6.0 / (C + C)).astype(np.float32)

        def w(k):
            return jax.random.uniform(k, (C, C), dtype=jnp.float32, minval=-lim, maxval=lim)
        return {'x': x, 'Wq': w(ks[1]), 'bq': jnp.zeros((C,), jnp.float32), 'Wk': w(ks[2]), 'bk': jnp.zeros((C,), jnp.float32), 'Wv': w(ks[3]), 'bv': jnp.zeros((C,), jnp.float32), 'Wo': w(ks[4]), 'bo': jnp.zeros((C,), jnp.float32)}
    _L0_attn_all = _L0_attn_setup()
    _L0_attn_in = {k: v for k, v in _L0_attn_all.items() if k in ('Wq', 'bq', 'Wk', 'bk', 'Wv', 'bv', 'Wo', 'bo')}
    del _L0_attn_all

    def _L0_ffn_setup():
        import jax, jax.numpy as jnp
        import numpy as np
        B, T, C = (64, 96, 64)
        NH, NKV = (4, 2)
        HD = C // NH
        NREP = NH // NKV
        NE, TOPK = (8, 2)
        HID = int(8 / 3 * C)
        EPS_RMS = 1e-06

        def _rope_tables(t_len):
            inv_freq = 1.0 / 10000.0 ** (np.arange(0, HD, 2, dtype=np.float32) / HD)
            t = np.arange(t_len, dtype=np.float32)
            freqs = np.outer(t, inv_freq)
            emb = np.concatenate([freqs, freqs], axis=-1)
            return (jnp.asarray(np.cos(emb)), jnp.asarray(np.sin(emb)))

        def _rotate_half(x):
            h = x.shape[-1] // 2
            return jnp.concatenate([-x[..., h:], x[..., :h]], axis=-1)

        def _rmsnorm(v, w):
            return v * jax.lax.rsqrt(jnp.mean(v * v, axis=-1, keepdims=True) + EPS_RMS) * w
        key = jax.random.key(seed)
        ks = jax.random.split(key, 10)
        s = lambda k, shape: jax.random.normal(k, shape, jnp.float32) * 0.02
        return {'x': jax.random.normal(ks[0], (B, T, C), jnp.float32), 'ln1_w': jnp.ones((C,), jnp.float32), 'ln2_w': jnp.ones((C,), jnp.float32), 'wq': s(ks[1], (NH * HD, C)), 'wk': s(ks[2], (NKV * HD, C)), 'wv': s(ks[3], (NKV * HD, C)), 'wo': s(ks[4], (C, C)), 'router_w': s(ks[5], (NE, C)), 'w1': s(ks[6], (NE, HID, C)), 'w2': s(ks[7], (NE, C, HID)), 'w3': s(ks[8], (NE, HID, C))}
    _L0_ffn_all = _L0_ffn_setup()
    _L0_ffn_in = {k: v for k, v in _L0_ffn_all.items() if k in ('ln1_w', 'ln2_w', 'wq', 'wk', 'wv', 'wo', 'router_w', 'w1', 'w2', 'w3')}
    del _L0_ffn_all

    def _L1_attn_setup():
        import jax, jax.numpy as jnp
        import numpy as np
        HEAD_SIZE = 64
        HEAD_SIZE_R = HEAD_SIZE // 4
        HEAD_SIZE_C = HEAD_SIZE - HEAD_SIZE_R
        N_EMBD = 64

        def rope(x, start_pos=0):
            B, T, d = x.shape
            half = d // 2
            theta = 1.0 / 10000.0 ** (jnp.arange(half, dtype=x.dtype) / half)
            idx = jnp.arange(start_pos, start_pos + T, dtype=x.dtype)[:, None] * theta[None, :]
            sin, cos = (jnp.sin(idx), jnp.cos(idx))
            xs = x.reshape(B, T, half, 2)
            x1, x2 = (xs[..., 0], xs[..., 1])
            rot = jnp.stack([x1 * cos - x2 * sin, x1 * sin + x2 * cos], axis=-1)
            return rot.reshape(B, T, d)

        def _reference_tuple_inner(x, Wq_comp, Wkv_comp, Wqc, Wqr, Wkc, Wkr, Wv):
            c_q = x @ Wq_comp
            c_kv = x @ Wkv_comp
            q_c = c_q @ Wqc
            q_r = rope(c_q @ Wqr, start_pos=0)
            q = jnp.concatenate([q_c, q_r], axis=-1)
            k_c = c_kv @ Wkc
            k_r = rope(c_kv @ Wkr, start_pos=0)
            k = jnp.concatenate([k_c, k_r], axis=-1)
            v = c_kv @ Wv
            scale = 1.0 / jnp.sqrt(jnp.asarray(HEAD_SIZE, dtype=x.dtype))
            wei = jnp.einsum('bqd,bkd->bqk', q, k) * scale
            T_q = q.shape[1]
            mask = jnp.tril(jnp.ones((T_q, T_q), dtype=bool))
            wei = jnp.where(mask, wei, jnp.asarray(-jnp.inf, dtype=wei.dtype))
            wei = jax.nn.softmax(wei, axis=-1)
            out = jnp.einsum('bqk,bkd->bqd', wei, v)
            return (out, (k, v))
        key = jax.random.key(seed)
        ks = jax.random.split(key, 8)
        B, T = (32, 512)
        s = 0.05
        return {'x': jax.random.normal(ks[0], (B, T, N_EMBD), dtype=jnp.float32), 'Wq_comp': jax.random.normal(ks[1], (N_EMBD, N_EMBD), dtype=jnp.float32) * s, 'Wkv_comp': jax.random.normal(ks[2], (N_EMBD, N_EMBD), dtype=jnp.float32) * s, 'Wqc': jax.random.normal(ks[3], (N_EMBD, HEAD_SIZE_C), dtype=jnp.float32) * s, 'Wqr': jax.random.normal(ks[4], (N_EMBD, HEAD_SIZE_R), dtype=jnp.float32) * s, 'Wkc': jax.random.normal(ks[5], (N_EMBD, HEAD_SIZE_C), dtype=jnp.float32) * s, 'Wkr': jax.random.normal(ks[6], (N_EMBD, HEAD_SIZE_R), dtype=jnp.float32) * s, 'Wv': jax.random.normal(ks[7], (N_EMBD, HEAD_SIZE), dtype=jnp.float32) * s}
    _L1_attn_all = _L1_attn_setup()
    _L1_attn_in = {k: v for k, v in _L1_attn_all.items() if k in ('Wq_comp', 'Wkv_comp', 'Wqc', 'Wqr', 'Wkc', 'Wkr', 'Wv')}
    del _L1_attn_all

    def _L1_ffn_setup():
        import jax, jax.numpy as jnp
        import numpy as np
        B, S, H, NH, NE = (4, 256, 64, 4, 4)
        D = H // NH
        EPS = 1e-08

        def layernorm(x, g, b):
            m = jnp.mean(x, axis=-1, keepdims=True)
            v = jnp.mean((x - m) ** 2, axis=-1, keepdims=True)
            return (x - m) / jnp.sqrt(v + EPS) * g + b
        key = jax.random.key(seed)
        ks = jax.random.split(key, 18)
        sc = 0.05
        return {'x': jax.random.normal(ks[0], (B, S, H), jnp.float32), 'hl_w': jax.random.normal(ks[1], (NH, D, H), jnp.float32) * sc, 'hl_b': jax.random.normal(ks[2], (NH, D), jnp.float32) * sc, 'wq': jax.random.normal(ks[3], (NH, NE, D, D), jnp.float32) * sc, 'wk': jax.random.normal(ks[4], (NH, D, D), jnp.float32) * sc, 'wv': jax.random.normal(ks[5], (NH, D, D), jnp.float32) * sc, 'gate_w': jax.random.normal(ks[6], (NH, NE, NE * D), jnp.float32) * sc, 'gate_b': jax.random.normal(ks[7], (NH, NE), jnp.float32) * sc, 'ln_g': jnp.ones((D,), jnp.float32), 'ln_b': jnp.zeros((D,), jnp.float32), 'fc1_w': jax.random.normal(ks[8], (D, D), jnp.float32) * sc, 'fc1_b': jax.random.normal(ks[9], (D,), jnp.float32) * sc, 'fc2_w': jax.random.normal(ks[10], (D, D), jnp.float32) * sc, 'fc2_b': jax.random.normal(ks[11], (D,), jnp.float32) * sc, 'fnorm_g': jnp.ones((D,), jnp.float32), 'fnorm_b': jnp.zeros((D,), jnp.float32), 'fgate_w': jax.random.normal(ks[12], (NH, H), jnp.float32) * sc}
    _L1_ffn_all = _L1_ffn_setup()
    _L1_ffn_in = {k: v for k, v in _L1_ffn_all.items() if k in ('hl_w', 'hl_b', 'wq', 'wk', 'wv', 'gate_w', 'gate_b', 'ln_g', 'ln_b', 'fc1_w', 'fc1_b', 'fc2_w', 'fc2_b', 'fnorm_g', 'fnorm_b', 'fgate_w')}
    del _L1_ffn_all
    return {'x': x, 'txt': txt, 'L0_tok_conv1_w': _L0_tok_in['conv1_w'], 'L0_tok_conv1_b': _L0_tok_in['conv1_b'], 'L0_tok_bn_gamma': _L0_tok_in['bn_gamma'], 'L0_tok_bn_beta': _L0_tok_in['bn_beta'], 'L0_tok_bn_mean': _L0_tok_in['bn_mean'], 'L0_tok_bn_var': _L0_tok_in['bn_var'], 'L0_tok_conv2_w': _L0_tok_in['conv2_w'], 'L0_tok_conv2_b': _L0_tok_in['conv2_b'], 'L0_attn_Wq': _L0_attn_in['Wq'], 'L0_attn_bq': _L0_attn_in['bq'], 'L0_attn_Wk': _L0_attn_in['Wk'], 'L0_attn_bk': _L0_attn_in['bk'], 'L0_attn_Wv': _L0_attn_in['Wv'], 'L0_attn_bv': _L0_attn_in['bv'], 'L0_attn_Wo': _L0_attn_in['Wo'], 'L0_attn_bo': _L0_attn_in['bo'], 'L0_ffn_ln1_w': _L0_ffn_in['ln1_w'], 'L0_ffn_ln2_w': _L0_ffn_in['ln2_w'], 'L0_ffn_wq': _L0_ffn_in['wq'], 'L0_ffn_wk': _L0_ffn_in['wk'], 'L0_ffn_wv': _L0_ffn_in['wv'], 'L0_ffn_wo': _L0_ffn_in['wo'], 'L0_ffn_router_w': _L0_ffn_in['router_w'], 'L0_ffn_w1': _L0_ffn_in['w1'], 'L0_ffn_w2': _L0_ffn_in['w2'], 'L0_ffn_w3': _L0_ffn_in['w3'], 'L1_attn_Wq_comp': _L1_attn_in['Wq_comp'], 'L1_attn_Wkv_comp': _L1_attn_in['Wkv_comp'], 'L1_attn_Wqc': _L1_attn_in['Wqc'], 'L1_attn_Wqr': _L1_attn_in['Wqr'], 'L1_attn_Wkc': _L1_attn_in['Wkc'], 'L1_attn_Wkr': _L1_attn_in['Wkr'], 'L1_attn_Wv': _L1_attn_in['Wv'], 'L1_ffn_hl_w': _L1_ffn_in['hl_w'], 'L1_ffn_hl_b': _L1_ffn_in['hl_b'], 'L1_ffn_wq': _L1_ffn_in['wq'], 'L1_ffn_wk': _L1_ffn_in['wk'], 'L1_ffn_wv': _L1_ffn_in['wv'], 'L1_ffn_gate_w': _L1_ffn_in['gate_w'], 'L1_ffn_gate_b': _L1_ffn_in['gate_b'], 'L1_ffn_ln_g': _L1_ffn_in['ln_g'], 'L1_ffn_ln_b': _L1_ffn_in['ln_b'], 'L1_ffn_fc1_w': _L1_ffn_in['fc1_w'], 'L1_ffn_fc1_b': _L1_ffn_in['fc1_b'], 'L1_ffn_fc2_w': _L1_ffn_in['fc2_w'], 'L1_ffn_fc2_b': _L1_ffn_in['fc2_b'], 'L1_ffn_fnorm_g': _L1_ffn_in['fnorm_g'], 'L1_ffn_fnorm_b': _L1_ffn_in['fnorm_b'], 'L1_ffn_fgate_w': _L1_ffn_in['fgate_w']}

def reference(x, txt, L0_tok_conv1_w, L0_tok_conv1_b, L0_tok_bn_gamma, L0_tok_bn_beta, L0_tok_bn_mean, L0_tok_bn_var, L0_tok_conv2_w, L0_tok_conv2_b, L0_attn_Wq, L0_attn_bq, L0_attn_Wk, L0_attn_bk, L0_attn_Wv, L0_attn_bv, L0_attn_Wo, L0_attn_bo, L0_ffn_ln1_w, L0_ffn_ln2_w, L0_ffn_wq, L0_ffn_wk, L0_ffn_wv, L0_ffn_wo, L0_ffn_router_w, L0_ffn_w1, L0_ffn_w2, L0_ffn_w3, L1_attn_Wq_comp, L1_attn_Wkv_comp, L1_attn_Wqc, L1_attn_Wqr, L1_attn_Wkc, L1_attn_Wkr, L1_attn_Wv, L1_ffn_hl_w, L1_ffn_hl_b, L1_ffn_wq, L1_ffn_wk, L1_ffn_wv, L1_ffn_gate_w, L1_ffn_gate_b, L1_ffn_ln_g, L1_ffn_ln_b, L1_ffn_fc1_w, L1_ffn_fc1_b, L1_ffn_fc2_w, L1_ffn_fc2_b, L1_ffn_fnorm_g, L1_ffn_fnorm_b, L1_ffn_fgate_w):
    import jax
    import jax.numpy as jnp

    def _L0_tok_ref(x, conv1_w, conv1_b, bn_gamma, bn_beta, bn_mean, bn_var, conv2_w, conv2_b):
        import jax, jax.numpy as jnp
        import numpy as np
        K = 3
        PAD = (K - 1) // 2
        BN_EPS = 1e-05

        def _unfold(x):
            b, c, h, w = x.shape
            xp = jnp.pad(x, ((0, 0), (0, 0), (PAD, PAD), (PAD, PAD)))
            shifts = [xp[:, :, i:i + h, j:j + w] for i in range(K) for j in range(K)]
            return jnp.stack(shifts, axis=2)
        b, c, h, w = x.shape
        y = jnp.einsum('oc,bchw->bohw', conv1_w, x) + conv1_b[None, :, None, None]
        y = (y - bn_mean[None, :, None, None]) * (bn_gamma[None, :, None, None] * jax.lax.rsqrt(bn_var + BN_EPS)[None, :, None, None]) + bn_beta[None, :, None, None]
        y = jax.nn.relu(y)
        wdyn = jnp.einsum('ok,bkhw->bohw', conv2_w, y) + conv2_b[None, :, None, None]
        patches = _unfold(x)
        out = jnp.einsum('bckhw,bkhw->bchw', patches, wdyn)
        return out.reshape(b, h * w, c)

    def _L0_attn_ref(x, Wq, bq, Wk, bk, Wv, bv, Wo, bo):
        import jax, jax.numpy as jnp
        import numpy as np
        DIM = 64
        HEADS = 4
        HEAD_DIM = DIM // HEADS
        SCALE = HEAD_DIM ** (-0.5)
        B, N, C = x.shape
        x = jnp.clip(x, -10000.0, 10000.0)

        def heads(t):
            return t.reshape(B, N, HEADS, HEAD_DIM).transpose(0, 2, 1, 3)
        q = heads((x @ Wq.T + bq).astype(jnp.float32))
        k = heads((x @ Wk.T + bk).astype(jnp.float32))
        v = heads((x @ Wv.T + bv).astype(jnp.float32))
        attn = jnp.einsum('bhnd,bhmd->bhnm', q, k) * SCALE
        attn = jax.nn.softmax(attn, axis=-1)
        out = jnp.einsum('bhnm,bhmd->bhnd', attn, v)
        out = out.transpose(0, 2, 1, 3).reshape(B, N, C)
        out = out.astype(jnp.bfloat16).astype(jnp.float32)
        return out @ Wo.T + bo

    def _L0_ffn_ref(x, ln1_w, ln2_w, wq, wk, wv, wo, router_w, w1, w2, w3):
        import jax, jax.numpy as jnp
        import numpy as np
        B, T, C = (64, 96, 64)
        NH, NKV = (4, 2)
        HD = C // NH
        NREP = NH // NKV
        NE, TOPK = (8, 2)
        HID = int(8 / 3 * C)
        EPS_RMS = 1e-06

        def _rope_tables(t_len):
            inv_freq = 1.0 / 10000.0 ** (np.arange(0, HD, 2, dtype=np.float32) / HD)
            t = np.arange(t_len, dtype=np.float32)
            freqs = np.outer(t, inv_freq)
            emb = np.concatenate([freqs, freqs], axis=-1)
            return (jnp.asarray(np.cos(emb)), jnp.asarray(np.sin(emb)))

        def _rotate_half(x):
            h = x.shape[-1] // 2
            return jnp.concatenate([-x[..., h:], x[..., :h]], axis=-1)

        def _rmsnorm(v, w):
            return v * jax.lax.rsqrt(jnp.mean(v * v, axis=-1, keepdims=True) + EPS_RMS) * w
        Bx, Tx, Cx = x.shape
        h = _rmsnorm(x, ln1_w)
        q = (h @ wq.T).reshape(Bx, Tx, NH, HD).transpose(0, 2, 1, 3)
        k = (h @ wk.T).reshape(Bx, Tx, NKV, HD).transpose(0, 2, 1, 3)
        v = (h @ wv.T).reshape(Bx, Tx, NKV, HD).transpose(0, 2, 1, 3)
        cos, sin = _rope_tables(Tx)
        cos, sin = (cos[None, None], sin[None, None])
        q = q * cos + _rotate_half(q) * sin
        k = k * cos + _rotate_half(k) * sin
        k = jnp.repeat(k, NREP, axis=1)
        v = jnp.repeat(v, NREP, axis=1)
        scores = jnp.einsum('bhtd,bhsd->bhts', q, k) / jnp.sqrt(jnp.float32(HD))
        causal = jnp.tril(jnp.ones((Tx, Tx), dtype=bool))
        scores = jnp.where(causal[None, None], scores, jnp.float32(-1e+30))
        att = jax.nn.softmax(scores, axis=-1)
        y = jnp.einsum('bhts,bhsd->bhtd', att, v).transpose(0, 2, 1, 3).reshape(Bx, Tx, Cx)
        x = x + y @ wo.T
        flat = _rmsnorm(x, ln2_w).reshape(-1, Cx)
        probs = jax.nn.softmax(flat @ router_w.T, axis=-1)
        tp, ti = jax.lax.top_k(probs, TOPK)
        tp = tp / (jnp.sum(tp, axis=-1, keepdims=True) + 1e-09)
        weights = jnp.sum(tp[..., None] * jax.nn.one_hot(ti, NE, dtype=flat.dtype), axis=1)
        out = jnp.zeros_like(flat)
        for e in range(NE):
            hh = jax.nn.silu(flat @ w1[e].T) * (flat @ w3[e].T)
            out = out + weights[:, e:e + 1] * (hh @ w2[e].T)
        return x + out.reshape(Bx, Tx, Cx)

    def _L1_attn_ref(x, Wq_comp, Wkv_comp, Wqc, Wqr, Wkc, Wkr, Wv):
        import jax, jax.numpy as jnp
        import numpy as np
        HEAD_SIZE = 64
        HEAD_SIZE_R = HEAD_SIZE // 4
        HEAD_SIZE_C = HEAD_SIZE - HEAD_SIZE_R
        N_EMBD = 64

        def rope(x, start_pos=0):
            B, T, d = x.shape
            half = d // 2
            theta = 1.0 / 10000.0 ** (jnp.arange(half, dtype=x.dtype) / half)
            idx = jnp.arange(start_pos, start_pos + T, dtype=x.dtype)[:, None] * theta[None, :]
            sin, cos = (jnp.sin(idx), jnp.cos(idx))
            xs = x.reshape(B, T, half, 2)
            x1, x2 = (xs[..., 0], xs[..., 1])
            rot = jnp.stack([x1 * cos - x2 * sin, x1 * sin + x2 * cos], axis=-1)
            return rot.reshape(B, T, d)

        def _reference_tuple_inner(x, Wq_comp, Wkv_comp, Wqc, Wqr, Wkc, Wkr, Wv):
            c_q = x @ Wq_comp
            c_kv = x @ Wkv_comp
            q_c = c_q @ Wqc
            q_r = rope(c_q @ Wqr, start_pos=0)
            q = jnp.concatenate([q_c, q_r], axis=-1)
            k_c = c_kv @ Wkc
            k_r = rope(c_kv @ Wkr, start_pos=0)
            k = jnp.concatenate([k_c, k_r], axis=-1)
            v = c_kv @ Wv
            scale = 1.0 / jnp.sqrt(jnp.asarray(HEAD_SIZE, dtype=x.dtype))
            wei = jnp.einsum('bqd,bkd->bqk', q, k) * scale
            T_q = q.shape[1]
            mask = jnp.tril(jnp.ones((T_q, T_q), dtype=bool))
            wei = jnp.where(mask, wei, jnp.asarray(-jnp.inf, dtype=wei.dtype))
            wei = jax.nn.softmax(wei, axis=-1)
            out = jnp.einsum('bqk,bkd->bqd', wei, v)
            return (out, (k, v))
        return _reference_tuple_inner(x, Wq_comp, Wkv_comp, Wqc, Wqr, Wkc, Wkr, Wv)[0]

    def _L1_ffn_ref(x, hl_w, hl_b, wq, wk, wv, gate_w, gate_b, ln_g, ln_b, fc1_w, fc1_b, fc2_w, fc2_b, fnorm_g, fnorm_b, fgate_w):
        import jax, jax.numpy as jnp
        import numpy as np
        B, S, H, NH, NE = (4, 256, 64, 4, 4)
        D = H // NH
        EPS = 1e-08

        def layernorm(x, g, b):
            m = jnp.mean(x, axis=-1, keepdims=True)
            v = jnp.mean((x - m) ** 2, axis=-1, keepdims=True)
            return (x - m) / jnp.sqrt(v + EPS) * g + b
        b, s, h = x.shape
        nh, d, _ = wk.shape
        ne = wq.shape[1]
        sx = jnp.einsum('bsh,ndh->bnsd', x, hl_w) + hl_b[None, :, None, :]
        pad = sx == 0
        q = jnp.einsum('bnsd,neod->bneso', sx, wq)
        k = jnp.einsum('bnsd,nod->bnso', sx, wk)
        v = jnp.einsum('bnsd,nod->bnso', sx, wv)
        causal = jnp.where(jnp.tril(jnp.ones((s, s), bool)), 0.0, -jnp.inf).astype(x.dtype)
        scores = jnp.einsum('bnesd,bntd->bnest', q, k) * d ** 0.5 + causal
        att = jax.nn.softmax(scores, axis=-1)
        qkv = jnp.einsum('bnest,bntd->bnesd', att, v)
        qkv = jnp.where(pad[:, :, None], 0.0, qkv)
        out = jnp.transpose(qkv, (0, 1, 3, 2, 4)).reshape(b, nh, s, ne * d)
        gs = jax.nn.softmax(jnp.einsum('bnsf,nef->bnse', out, gate_w) + gate_b[None, :, None, :], axis=-1)
        mixed = jnp.einsum('bnsed,bnse->bnsd', out.reshape(b, nh, s, ne, d), gs)
        resid = sx[jnp.arange(nh), jnp.arange(nh)]
        hn = layernorm(mixed + resid, ln_g, ln_b)
        f_n = jnp.transpose(hn, (0, 2, 1, 3)).reshape(b, s, h)
        fx = f_n.reshape(b, s, nh, d)
        pm = fx == 0
        hx = jnp.where(pm, 0.0, fx @ fc1_w.T + fc1_b)
        hx = jax.nn.relu(hx)
        hx = jnp.where(pm, 0.0, hx @ fc2_w.T + fc2_b)
        hx = layernorm(hx + fx, fnorm_g, fnorm_b)
        fout = hx.reshape(b, s, h)
        fg = jax.nn.softmax(fout @ fgate_w.T, axis=-1)
        return (fout.reshape(b, s, nh, d) * fg[..., None]).reshape(b, s, h)
    h = _L0_tok_ref(x, L0_tok_conv1_w, L0_tok_conv1_b, L0_tok_bn_gamma, L0_tok_bn_beta, L0_tok_bn_mean, L0_tok_bn_var, L0_tok_conv2_w, L0_tok_conv2_b)
    h = jnp.concatenate([h, txt], axis=1)
    h = h + _L0_attn_ref(_layernorm(h, axis=-1), L0_attn_Wq, L0_attn_bq, L0_attn_Wk, L0_attn_bk, L0_attn_Wv, L0_attn_bv, L0_attn_Wo, L0_attn_bo)
    h = h + _L0_ffn_ref(_layernorm(h, axis=-1), L0_ffn_ln1_w, L0_ffn_ln2_w, L0_ffn_wq, L0_ffn_wk, L0_ffn_wv, L0_ffn_wo, L0_ffn_router_w, L0_ffn_w1, L0_ffn_w2, L0_ffn_w3)
    h = h + _L1_attn_ref(_layernorm(h, axis=-1), L1_attn_Wq_comp, L1_attn_Wkv_comp, L1_attn_Wqc, L1_attn_Wqr, L1_attn_Wkc, L1_attn_Wkr, L1_attn_Wv)
    h = h + _L1_ffn_ref(_layernorm(h, axis=-1), L1_ffn_hl_w, L1_ffn_hl_b, L1_ffn_wq, L1_ffn_wk, L1_ffn_wv, L1_ffn_gate_w, L1_ffn_gate_b, L1_ffn_ln_g, L1_ffn_ln_b, L1_ffn_fc1_w, L1_ffn_fc1_b, L1_ffn_fc2_w, L1_ffn_fc2_b, L1_ffn_fnorm_g, L1_ffn_fnorm_b, L1_ffn_fgate_w)
    return h

_drawn_inputs = setup_inputs


def setup_inputs(seed=0):
    import zlib

    import numpy as np

    out = dict(_drawn_inputs(seed))
    spreads = {'L0_tok_conv1_b': (0.0, 0.1),
     'L0_tok_bn_gamma': (1.0, 0.2),
     'L0_tok_bn_beta': (0.0, 0.1),
     'L0_tok_bn_mean': (0.0, 0.1),
     'L0_tok_bn_var': (1.0, 0.2),
     'L0_tok_conv2_b': (0.0, 0.1),
     'L0_attn_bq': (0.0, 0.8),
     'L0_attn_bk': (0.0, 2.0),
     'L0_attn_bv': (0.0, 0.1),
     'L0_attn_bo': (0.0, 0.1),
     'L0_ffn_ln1_w': (1.0, 0.6),
     'L0_ffn_ln2_w': (1.0, 0.6),
     'L1_ffn_ln_g': (1.0, 0.6),
     'L1_ffn_ln_b': (0.0, 2.0),
     'L1_ffn_fnorm_g': (1.0, 0.6),
     'L1_ffn_fnorm_b': (0.0, 2.0)}
    factors = {'L0_ffn_wq': 8.0,
     'L0_ffn_wk': 8.0,
     'L0_ffn_wv': 8.0,
     'L0_ffn_wo': 8.0,
     'L0_ffn_router_w': 8.0,
     'L0_ffn_w1': 8.0,
     'L0_ffn_w2': 8.0,
     'L0_ffn_w3': 8.0,
     'L1_attn_Wq_comp': 8.0,
     'L1_attn_Wkv_comp': 8.0,
     'L1_attn_Wqc': 8.0,
     'L1_attn_Wqr': 8.0,
     'L1_attn_Wkc': 8.0,
     'L1_attn_Wkr': 8.0,
     'L1_attn_Wv': 8.0,
     'L1_ffn_hl_b': 14.899,
     'L1_ffn_wq': 32.699,
     'L1_ffn_wk': 29.721,
     'L1_ffn_wv': 25.362,
     'L1_ffn_gate_w': 41.243,
     'L1_ffn_gate_b': 64.0,
     'L1_ffn_fc1_w': 24.035,
     'L1_ffn_fc1_b': 64.0,
     'L1_ffn_fc2_w': 8.0,
     'L1_ffn_fc2_b': 64.0,
     'L1_ffn_hl_w': 3.157,
     'L1_ffn_fgate_w': 5.421}
    for name, (base, spread) in spreads.items():
        noise = np.random.default_rng([zlib.crc32(name.encode()), seed]).standard_normal(out[name].shape)
        drawn = base * np.exp(spread * noise) if base else spread * noise
        out[name] = jnp.asarray(drawn.astype(out[name].dtype))
    for name, factor in factors.items():
        out[name] = (out[name] * factor).astype(out[name].dtype)
    return out
```

```python
from contextlib import ExitStack

import concourse.bass as bass
from concourse import mybir

F32 = mybir.dt.float32
BF16 = mybir.dt.bfloat16
ALU = mybir.AluOpType
ACT = mybir.ActivationFunctionType
AX = mybir.AxisListType.X

P = 128
B = 2
C = 64
IMG = 64
NT = 33
T = NT * P
L = 3
NTRIO = NT // L
W3 = L * P
D = 16
SLOTS = 6
KQ = SLOTS * D
NE, HID = 8, 170
HH = HID // 2
LN_EPS = 1e-5
NEG = -1e30

BANK_MAX = 0
BANK_EXP = 3
BANK_OUT = 6
BANK_ROW = 7


class Layer:

    def __init__(self, name, kv, rep, causal, dv, units, qscale):
        self.name, self.kv, self.rep, self.causal, self.dv, self.units = name, kv, rep, causal, dv, units
        self.qscale = qscale
        self.heads = kv * rep
        self.trios = [(j + 1) if causal else NTRIO for j in range(NTRIO)]
        self.steps = L * sum(self.trios)
        self.first = [L * sum(self.trios[:j]) for j in range(NTRIO)]
        self.wide = dv == C
        self.planes = 3 if self.wide else 1
        self.nq = 4 * D if self.wide else self.heads * D
        self.nk = 4 * D if self.wide else kv * D
        self.w = dv + 1


ATT0 = Layer("a0", 4, 1, False, D, B, D ** -0.5)
ATT1 = Layer("a1", 2, 2, True, D, B, D ** -0.5)
ATT2 = Layer("a2", 1, 1, True, C, B, C ** -0.5)
ATT3 = Layer("a3", 1, 4, True, D, B * 4, D ** 0.5)


def weight_columns():
    at, out = 0, {}
    for name, n in (("conv1", 16), ("bn", 5), ("conv2", 9), ("wqkv0", 192), ("wo0", 64), ("ln1", 1), ("ln2", 1),
                    ("wqkv1", 128), ("wo1", 64), ("router", NE), ("w1", NE * HID), ("w3", NE * HID),
                    ("w2", 2 * NE * C), ("wcomp", 128), ("wsec", 192), ("hl", 64), ("wn", 4 * 96),
                    ("gate", 16), ("gateb", 16), ("lng", D), ("lnb", D), ("fc1", 64), ("fc2", 64),
                    ("fng", D), ("fnb", D), ("fgate", 4)):
        out[name] = (at, n)
        at += n
    return out, at


COLS, NCOLS = weight_columns()


def build(nc, x, txt, wpack, rope0, rope1, wd_scratch, out):
    outer = ExitStack()
    with outer:
        def sb(name, shape, dt, ctx=outer):
            return ctx.enter_context(nc.sbuf_tensor(name, shape, dt))

        sems = {}

        def sem(name):
            if name not in sems:
                sems[name] = outer.enter_context(nc.semaphore(name))
            return sems[name]

        PS = outer.enter_context(nc.psum_tensor("PS", [P, 8, 512], F32))
        PSH = PS[:, :, :].rearrange("p a b -> p (a b)").bitcast(BF16)

        H = sb("H", [P, B * NT, C], F32)
        WP = sb("WP", [P, NCOLS], F32)
        XN = sb("XN", [P, NT, C], F32)
        XT = sb("XT", [C + 1, W3], F32)
        identf = sb("identf", [P, P], F32)
        identh = sb("identh", [P, P], BF16)
        maskq = sb("maskq", [P, P], BF16)
        maskk = sb("maskk", [P, P], BF16)
        ones2 = sb("ones2", [2, P], BF16)
        st = sb("st", [P, 4, NT], F32)
        bnv = sb("bnv", [16, 4], F32)
        MH = sb("MH", [P, NT], F32)

        def wt(name, rows, a=0, n=None):
            at, cols = COLS[name]
            return WP[0:rows, at + a:at + a + (cols - a if n is None else n)]

        tok = ExitStack()
        XC = sb("XC", [C, B, IMG * IMG], F32, tok)
        XS = sb("XS", [P, L, 32, IMG + 2], F32, tok)
        YC = sb("YC", [17, IMG * IMG], F32, tok)
        WD = sb("WD", [9, IMG * IMG], F32, tok)
        WB = sb("WB", [P, 9, IMG], F32, tok)
        TM = sb("TM", [P, 2, 32, IMG], F32, tok)
        tok.close()

        QT = sb("QT", [P, 4, T], BF16)
        KT = sb("KT", [P, 4, T], BF16)
        V = sb("V", [P, NT * 4 * (D + 1)], F32)
        Y = sb("Y", [P, NT, 256], F32)
        SX = sb("SX", [P, B * NT, C], F32)
        PT = sb("PT", [P, L, W3], F32)
        PM = sb("PM", [P, L, NTRIO], F32)
        NM = sb("NM", [P, L], F32)
        MM = sb("MM", [P, L, 2], BF16)
        RC = sb("RC", [P, L], F32)
        STG = sb("STG", [P, L, C], F32)
        YB = sb("YB", [P, L, C], BF16)
        CT = sb("CT", [P, W3], F32)
        QK = sb("QK", [P, L, P], F32)
        R1 = sb("R1", [P, L, P], F32)
        R2 = sb("R2", [P, L, P], F32)
        parts = sb("parts", [P, (SLOTS + 3) * W3 // 2], F32)
        halves = parts[:, :].bitcast(BF16)
        C01 = halves[:, 0:3 * W3].rearrange("p (a l c) -> p a l c", a=3, l=L)
        A = halves[:, 3 * W3:(SLOTS + 3) * W3].rearrange("p (l c) -> p l c", l=L)
        RT = sb("RT", [P, 2, NT, D], F32)
        G = parts[0:HH, 0:4 * W3].rearrange("p (a b c) -> p a b c", a=2, b=2)
        X1 = sb("X1", [P, L, C], F32)
        OM = sb("OM", [P, L, 256], F32)
        OT = PT[:, 0:2, :]
        E1 = sb("E1", [P, 8, L * C], F32)
        S1 = sb("S1", [P, 8, L * 16], F32)

        bars = [0]

        passed = sem("passed")

        def barrier(eng, k):
            eng.drain()
            eng.sem_inc(sem("met"), 1)
            eng.wait_ge(sem("met"), 4 * k)
            eng.sem_inc(passed, 1)

        MEET_TOK = 2
        BASE0 = MEET_TOK
        BASE1 = BASE0 + 1 + 3 * B
        BASE2 = BASE1 + 1 + 3 * B
        BASE3 = BASE2 + 1 + 3 * B
        MEET3 = 2 * 4 + 1

        def vflat(lay, kt, kvh):
            return V[:, bass.ds((kt * lay.kv + kvh) * lay.w, lay.w)]


        def s(lay, what):
            return sem(f"{lay.name}_{what}")

        def plan(lay, j):
            n = lay.trios[j]
            nxt = lay.trios[j + 1] if j + 1 < NTRIO else 0
            lead = nxt - n + 1 if nxt else 0
            if n == 1:
                return [(0, list(range(nxt)))]
            out_ = [(0, list(range(lead)))]
            out_ += [(t, [t + lead - 1] if nxt else []) for t in range(1, n)]
            return out_

        def share(nexts, r):
            every = [(t, lane) for t in nexts for lane in range(L)]
            return every[r * len(nexts):(r + 1) * len(nexts)]

        def pe_max(pe, lay, g0, h, kvh, j, t, lane):
            diag = lay.causal and isinstance(t, int) and t == lay.trios[j] - 1
            cols = (lane + 1) * P if diag else W3
            pe.wait_ge(s(lay, "maxbank_free"), g0 + lay.first[j] + t * L + lane + 1)
            for p in range(lay.planes):
                qp, kp = (p, p) if lay.wide else (h, kvh)
                k = P if lay.wide else KQ
                last = not diag and p == lay.planes - 1
                mm = pe.matmul(PS[:, BANK_MAX + lane, 0:cols],
                               QT[0:k].rearrange("p a t -> p (a t)")[:, bass.ds(qp * T + (L * j + lane) * P, P)],
                               KT[0:k].rearrange("p a t -> p (a t)")[:, bass.ds(kp * T + t * W3, cols)],
                               start=p == 0, stop=last, skip_group_check=True)
            if diag:
                mm = pe.matmul(PS[:, BANK_MAX + lane, lane * P:cols], identh[:, :], maskq[:, :],
                               start=False, stop=True, skip_group_check=True)
            mm.then_inc(s(lay, "maxscores"), 1)

        def pe_score(pe, lay, g0, h, kvh, j, t, r):
            diag = lay.causal and isinstance(t, int) and t == lay.trios[j] - 1
            c0 = r * P if diag else 0
            pe.wait_ge(s(lay, "exps"), g0 + lay.first[j] + t * L + r + 1)
            for p in range(lay.planes):
                qp, kp = (p, p) if lay.wide else (h, kvh)
                k = P if lay.wide else KQ + 2
                last = not diag and not lay.wide
                mm = pe.matmul(PS[:, BANK_EXP + r, c0:W3],
                               KT[0:k].rearrange("p a t -> p (a t)")[:, bass.ds(kp * T + (t * L + r) * P, P)],
                               QT[0:k].rearrange("p a t -> p (a t)")[:, bass.ds(qp * T + j * W3 + c0, W3 - c0)],
                               start=p == 0, stop=last, skip_group_check=True)
            if lay.wide:
                mm = pe.matmul(PS[:, BANK_EXP + r, c0:W3], ones2[:, :],
                               QT[0:2, 3, j * W3 + c0:(j + 1) * W3],
                               start=False, stop=not diag, skip_group_check=True)
            if diag:
                mm = pe.matmul(PS[:, BANK_EXP + r, c0:c0 + P], identh[:, :], maskk[:, :],
                               start=False, stop=True, skip_group_check=True)
            mm.then_inc(s(lay, "scores"), 1)

        def pe_values(pe, lay, g0, b0, kvh, j, t, r, first, last):
            diag = lay.causal and isinstance(t, int) and t == lay.trios[j] - 1
            l0 = r if diag else 0
            pe.wait_ge(s(lay, "exps"), g0 + lay.first[j] + t * L + r + 1 + L)
            if first:
                pe.wait_ge(s(lay, "out_free"), b0 + j + 1)
            for lane in range(l0, L):
                mm = pe.matmul(PS[:, BANK_OUT, lane * lay.w:(lane + 1) * lay.w], PT[:, r, lane * P:(lane + 1) * P],
                               vflat(lay, t * L + r, kvh), start=first and lane == 0, stop=last,
                               skip_group_check=True)
            mm.then_inc(s(lay, "values"), 1)

        def pe_maxrow(pe, lay, b0, j):
            pe.wait_ge(s(lay, "negmax"), b0 + j + 1)
            for lane in range(L):
                mm = pe.matmul(PS[0:2, BANK_ROW, lane * P:(lane + 1) * P], MM[:, lane, :], identh[:, :],
                               start=True, stop=True)
            mm.then_inc(s(lay, "maxrow"), 1)

        def pe_head(pe, lay, u, kvh, rr):
            h = kvh * lay.rep + rr
            g0 = (u * lay.heads + h) * lay.steps
            b0 = (u * lay.heads + h) * NTRIO
            if lay.causal:
                for lane in range(L):
                    pe_max(pe, lay, g0, h, kvh, 0, 0, lane)
            else:
                with pe.Fori(0, NTRIO) as t:
                    for lane in range(L):
                        pe_max(pe, lay, g0, h, kvh, 0, t, lane)
            pe_maxrow(pe, lay, b0, 0)
            for j in range(NTRIO):
                trios = plan(lay, j)
                n = len(trios)

                def trio(t, nexts, first):
                    for r in range(L):
                        for t2, lane in share(nexts, r):
                            pe_max(pe, lay, g0, h, kvh, j + 1, t2, lane)
                        if first and r == 0:
                            pe.wait_ge(s(lay, "maxrow_set"), b0 + j + 1)
                            pe.sem_inc(passed, 1)
                        pe_score(pe, lay, g0, h, kvh, j, t, r)
                        if r == 2:
                            pe_values(pe, lay, g0, b0, kvh, j, t, 0, first, False)
                        elif not first:
                            pe_values(pe, lay, g0, b0, kvh, j, t - 1, r + 1, False, False)
                        elif j > 0:
                            pe_values(pe, lay, g0, b0, kvh, j - 1, lay.trios[j - 1] - 1, r + 1, False, r == 1)

                trio(*trios[0], True)
                if n > 3:
                    shift = trios[1][1][0] - 1 if trios[1][1] else None
                    with pe.Fori(1, n - 1) as t:
                        trio(t, [t + shift] if shift is not None else [], False)
                    trio(*trios[-1], False)
                else:
                    for one in trios[1:]:
                        trio(*one, False)
                if j + 1 < NTRIO:
                    pe_maxrow(pe, lay, b0, j + 1)
            for r in (1, 2):
                pe_values(pe, lay, g0, b0, kvh, NTRIO - 1, lay.trios[-1] - 1, r, False, r == 2)

        def act_head(act, lay, u, kvh, rr):
            g0 = (u * lay.heads + kvh * lay.rep + rr) * lay.steps
            for j in range(NTRIO):
                n = lay.trios[j]

                def trio(t, diag):
                    for r in range(L):
                        c0 = r * P if diag else 0
                        g = g0 + lay.first[j] + t * L + r
                        act.wait_ge(s(lay, "scores"), g + 1)
                        act.wait_ge(s(lay, "values"), g + 1)
                        act.activation(PT[:, r, c0:W3], PS[:, BANK_EXP + r, c0:W3], ACT.Exp)\
                           .then_inc(s(lay, "exps"), 1)

                full = n - 1 if lay.causal else n
                if full > 1:
                    with act.Fori(0, full) as t:
                        trio(t, False)
                elif full == 1:
                    trio(0, False)
                if lay.causal:
                    trio(n - 1, True)

        def dve_max(dve, lay, g0, j, t, lane):
            diag = lay.causal and isinstance(t, int) and t == lay.trios[j] - 1
            cols = (lane + 1) * P if diag else W3
            dve.wait_ge(s(lay, "maxscores"), g0 + lay.first[j] + t * L + lane + 1)
            dve.tensor_reduce(PM[:, lane, bass.ds(t, 1)], PS[:, BANK_MAX + lane, 0:cols], AX, ALU.max)\
               .then_inc(s(lay, "maxbank_free"), 1)

        def dve_rows(dve, lay, b0, h, j):
            dve.drain()
            dve.tensor_reduce(NM[:, :], PM[:, :, 0:lay.trios[j]], AX, ALU.max, negate=True)
            dve.drain()
            dve.tensor_copy(MM[:, :, 0], NM[:, :])
            dve.drain()
            dve.tensor_tensor(MM[:, :, 1], NM[:, :], MM[:, :, 0], ALU.subtract).then_inc(s(lay, "negmax"), 1)
            dve.wait_ge(s(lay, "maxrow"), b0 + j + 1)
            if lay.wide:
                dst = QT[0:2, 3, j * W3:(j + 1) * W3]
            else:
                dst = QT[KQ:KQ + 2].rearrange("p a t -> p (a t)")[:, bass.ds(h * T + j * W3, W3)]
            dve.tensor_copy(dst, PS[0:2, BANK_ROW, 0:W3]).then_inc(s(lay, "maxrow_set"), 1)

        def dve_out(dve, lay, g0, h, j):
            dve.wait_ge(s(lay, "values"), g0 + lay.first[j] + L * lay.trios[j] + L)
            acc = PS[:, BANK_OUT, 0:L * lay.w].rearrange("p (l w) -> p l w", w=lay.w)
            dve.reciprocal(RC[:, :], acc[:, :, lay.dv])
            dve.drain()
            dve.tensor_tensor(Y[:, L * j:L * j + L, bass.ds(h * lay.dv, lay.dv)], acc[:, :, 0:lay.dv],
                              RC[:, :].unsqueeze(2).broadcast_to([P, L, lay.dv]), ALU.mult)\
               .then_inc(s(lay, "out_free"), 1)

        def dve_head(dve, lay, u, kvh, rr, yh):
            h = kvh * lay.rep + rr
            g0 = (u * lay.heads + h) * lay.steps
            b0 = (u * lay.heads + h) * NTRIO
            if lay.causal:
                for lane in range(L):
                    dve_max(dve, lay, g0, 0, 0, lane)
            else:
                with dve.Fori(0, NTRIO) as t:
                    for lane in range(L):
                        dve_max(dve, lay, g0, 0, t, lane)
            dve_rows(dve, lay, b0, h, 0)
            for j in range(NTRIO):
                trios = plan(lay, j)
                n = len(trios)
                for r in range(L):
                    for t2, lane in share(trios[0][1], r):
                        dve_max(dve, lay, g0, j + 1, t2, lane)
                    if r == 1 and j > 0:
                        dve_out(dve, lay, g0, yh, j - 1)
                if j + 1 < NTRIO and n > 1:
                    if n > 3:
                        shift = trios[1][1][0] - 1
                        with dve.Fori(1, n - 1) as t:
                            for lane in range(L):
                                dve_max(dve, lay, g0, j + 1, t + shift, lane)
                        for lane in range(L):
                            dve_max(dve, lay, g0, j + 1, trios[-1][1][0], lane)
                    else:
                        for _, nexts in trios[1:]:
                            for lane in range(L):
                                dve_max(dve, lay, g0, j + 1, nexts[0], lane)
                if j + 1 < NTRIO:
                    dve_rows(dve, lay, b0, h, j + 1)
            dve_out(dve, lay, g0, yh, NTRIO - 1)

        def heads(eng, lay, body):
            if lay.kv > 1 and lay.rep > 1:
                with eng.Fori(0, lay.kv) as kvh:
                    with eng.Fori(0, lay.rep) as rr:
                        body(kvh, rr)
            elif lay.kv > 1:
                with eng.Fori(0, lay.kv) as kvh:
                    body(kvh, 0)
            elif lay.rep > 1:
                with eng.Fori(0, lay.rep) as rr:
                    body(0, rr)
            else:
                body(0, 0)


        def ask_rstd(dve, what, k):
            dve.drain()
            dve.sem_inc(sem(what + "_var"), 1)
            dve.wait_ge(sem(what + "_rstd"), k + 1)
            dve.sem_inc(passed, 1)

        def pool_rstd(pool, what, k, n, eps):
            pool.wait_ge(sem(what + "_var"), k + 1)
            pool.sem_inc(passed, 1)
            pool.tensor_scalar(st[:, 1, 0:n], st[:, 3, 0:n], eps, None, ALU.add)
            pool.drain()
            pool.tensor_tensor(st[:, 2, 0:n], st[:, 1, 0:n], MH[:, 0:n], ALU.pow)\
                .then_inc(sem(what + "_rstd"), 1)

        def dve_layernorm(dve, b, what, sq):
            hb = H[:, bass.ds(b * NT, NT), :]
            dve.tensor_reduce(st[:, 0, :], hb, AX, ALU.add)
            dve.drain()
            dve.tensor_scalar(st[:, 1, :], st[:, 0, :], 1.0 / C, None, ALU.mult)
            dve.drain()
            dve.tensor_tensor(XN[:, :, :], hb, st[:, 1, :].unsqueeze(2).broadcast_to([P, NT, C]), ALU.subtract)
            dve.drain()
            dve.tensor_tensor(sq, XN[:, :, :], XN[:, :, :], ALU.mult)
            dve.drain()
            dve.tensor_reduce(st[:, 2, :], sq, AX, ALU.add)
            dve.drain()
            dve.tensor_scalar(st[:, 3, :], st[:, 2, :], 1.0 / C, None, ALU.mult)
            ask_rstd(dve, what, b)
            dve.tensor_tensor(XN[:, :, :], XN[:, :, :], st[:, 2, :].unsqueeze(2).broadcast_to([P, NT, C]), ALU.mult)
            dve.drain()

        def dve_split(dve, lay, it):
            n = lay.nq + lay.nk
            q, r1 = QK[:, :, 0:n], R1[:, :, 0:n]
            dve.tensor_copy(C01[:, 0, :, 0:n], q)
            dve.drain()
            dve.tensor_tensor(r1, q, C01[:, 0, :, 0:n], ALU.subtract)
            dve.drain()
            dve.tensor_copy(C01[:, 1, :, 0:n], r1)
            dve.drain()
            dve.tensor_tensor(C01[:, 2, :, 0:n], r1, C01[:, 1, :, 0:n], ALU.subtract).then_inc(s(lay, "parts"), 1)

        def pool_slots(pool, lay, it):
            nq, nk = lay.nq, lay.nk
            pool.wait_ge(s(lay, "parts"), it + 1)
            pool.sem_inc(passed, 1)
            d = C if lay.wide else D
            for c0, n, order in ((0, nq, (0, 0, 1, 1, 0, 2)), (nq, nk, (0, 1, 0, 1, 2, 0))):
                to = A[:, :, c0 * SLOTS:(c0 + n) * SLOTS].rearrange("p l (h s d) -> p l h s d", s=SLOTS, d=d)
                for slot, part in enumerate(order):
                    pool.tensor_copy(to[:, :, :, slot, :],
                                     C01[:, part, :, c0:c0 + n].rearrange("p l (h d) -> p l h d", d=d))
            pool.drain()
            pool.sem_inc(s(lay, "slots"), 1)

        def pe_turn(pe, lay, it):
            pe.wait_ge(s(lay, "slots"), it + 1)
            pe.sem_inc(passed, 1)
            for base, c0, n in ((4 * 1024, 0, lay.nq), (6 * 1024, lay.nq, lay.nk)):
                if lay.wide:
                    for p in range(3):
                        for l in range(L):
                            mm = pe.transpose(PSH[:, base + (p * L + l) * P:base + (p * L + l + 1) * P],
                                              A[:, l, c0 * SLOTS + p * P:c0 * SLOTS + (p + 1) * P], identh[:, :])
                else:
                    for i in range(n // D):
                        for l in range(L):
                            mm = pe.transpose(PSH[0:KQ, base + (i * L + l) * P:base + (i * L + l + 1) * P],
                                              A[:, l, c0 * SLOTS + i * KQ:c0 * SLOTS + (i + 1) * KQ], identh[:, :])
            mm.then_inc(s(lay, "turned"), 1)

        def put_turned(eng, lay, it, t, which):
            eng.wait_ge(s(lay, "turned"), it + 1)
            eng.sem_inc(passed, 1)
            rows = P if lay.wide else KQ
            n = 3 if lay.wide else (lay.nq if which == 0 else lay.nk) // D
            dst, base = (QT, 4 * 1024) if which == 0 else (KT, 6 * 1024)
            o = dst[0:rows, 0:n, bass.ds(t * W3, W3)]
            i = PSH[0:rows, base:base + n * W3].rearrange("p (a t) -> p a t", t=W3)
            if which == 0:
                eng.activation(o, i, ACT.Copy).then_inc(s(lay, "put"), 1)
            else:
                eng.tensor_copy(o, i).then_inc(s(lay, "put"), 1)

        def put_values(act, lay, t, c0):
            v = V[:, 0:NT * lay.kv * lay.w].rearrange("p (t k w) -> p t k w", k=lay.kv, w=lay.w)
            for l in range(L):
                last = act.activation(v[:, bass.ds(t * L + l, 1), :, 0:lay.dv].rearrange("p a k d -> p (a k) d"),
                                      PS[:, 1 + l, c0:c0 + lay.kv * lay.dv].rearrange("p (k d) -> p k d", d=lay.dv),
                                      ACT.Copy)
            return last

        block = outer.enter_context(nc.Block())

        @block.sync
        def _(sp):
            sp.dma_start(WP[:, :], wpack).then_inc(sem("weights_in"), 16)
            for b in range(B):
                sp.dma_start(XC[:, b, :], x[b].rearrange("c h w -> c (h w)")).then_inc(sem("image_in"), 16)
            for b in range(B):
                sp.dma_start(H[:, b * NT + NT - 1, :], txt[b]).then_inc(sem("text_in"), 16)
            xr = x.rearrange("b (t c) h w -> b c h t w", c=2)
            for b in range(B):
                sp.wait_ge(sem("shift_free"), b + 1)
                for i in range(3):
                    lo, hi = max(0, 1 - i), min(IMG, IMG + 1 - i)
                    for c2 in range(2):
                        for hf in range(2):
                            a_, z_ = (lo, 32) if hf == 0 else (32, hi)
                            for t0 in range(0, 32, 16):
                                sp.dma_start(XS[c2 * IMG + a_:c2 * IMG + z_, i, t0:t0 + 16, 1:IMG + 1],
                                             xr[b, c2, a_ + i - 1:z_ + i - 1, t0:t0 + 16, :])\
                                  .then_inc(sem("shift_in"), 16)
                sp.wait_ge(sem("dyn"), b + 1)
                sp.dma_start(wd_scratch[b], WD[:, :]).then_inc(sem("dyn_out"), 16)
                sp.wait_ge(sem("dyn_out"), 16 * (b + 1))
                for c2 in range(2):
                    sp.dma_start(WB[c2 * IMG:(c2 + 1) * IMG, :, :],
                                 wd_scratch[b].rearrange("k (h w) -> h k w", w=IMG)).then_inc(sem("rows_in"), 16)
            sp.wait_ge(sem("table_free"), 1)
            sp.dma_start(RT[:, :, :, :], rope0).then_inc(sem("table_in"), 16)
            sp.wait_ge(sem("table_free"), 2)
            sp.dma_start(RT[:, :, :, 0:D // 2], rope1).then_inc(sem("table_in"), 16)
            sp.wait_ge(sem("final"), 1)
            for b in range(B):
                sp.dma_start(out[b].rearrange("(t p) w -> p t w", p=P), H[:, b * NT:(b + 1) * NT, :])\
                  .then_inc(sem("stored"), 16)
            sp.wait_ge(sem("stored"), 16 * B)
            sp.wait_ge(sem("table_in"), 16 * 2)

        @block.gpsimd
        def _(pool):
            pool.wait_ge(sem("weights_in"), 16)
            pool.sem_inc(passed, 1)
            pool.memset(MH[:, :], -0.5)
            pool.tensor_scalar(bnv[:, 0:1], wt("bn", 16, 3, 1), 1e-5, None, ALU.add)
            pool.drain()
            pool.tensor_tensor(bnv[:, 2:3], bnv[:, 0:1], MH[0:16, 0:1], ALU.pow).then_inc(sem("bn_rstd"), 1)
            pool.memset(XS[:, :, :, :].rearrange("p a b c -> p (a b c)"), 0.0).then_inc(sem("shift_free"), 1)
            pool.memset(YC[:, :], 1.0).then_inc(sem("ones_row"), 1)
            pool.memset(identf[:, :], 0.0)
            pool.memset(maskq[:, :], 0.0)
            pool.memset(maskk[:, :], 0.0)
            pool.drain()
            pool.memset(ones2[:, :], 1.0)
            pool.drain()
            pool.memset(XT[C:C + 1, :], 1.0)
            pool.drain()
            pool.affine_select(out=identf[:, :], in_=identf[:, :], compare_op=ALU.not_equal, fill=1.0, base=0,
                               pattern=[[-1, P]], channel_multiplier=1)
            pool.affine_select(out=maskq[:, :], in_=maskq[:, :], compare_op=ALU.is_ge, fill=NEG, base=0,
                               pattern=[[-1, P]], channel_multiplier=1)
            pool.affine_select(out=maskk[:, :], in_=maskk[:, :], compare_op=ALU.is_ge, fill=NEG, base=0,
                               pattern=[[1, P]], channel_multiplier=-1)
            pool.drain()
            pool.tensor_copy(identh[:, :], identf[:, :])
            barrier(pool, 1)
            barrier(pool, 2)
            pool.sem_inc(sem("table_free"), 1)

            def ones(lay, k):
                pool.memset(V[:, :], 1.0)
                pool.drain()
                if not lay.wide:
                    pool.memset(KT[KQ:KQ + 2, 0:lay.kv, :], 1.0)
                barrier(pool, k)

            ones(ATT0, BASE0 + 1)
            with pool.Fori(0, B) as b:
                pool_rstd(pool, "ln0", b, NT, LN_EPS)
                with pool.Fori(0, NTRIO) as t:
                    pool_slots(pool, ATT0, b * NTRIO + t)
                for i in range(2):
                    barrier(pool, BASE0 + 2 + 3 * b + i)
                with pool.Fori(0, NTRIO) as t:
                    pool.wait_ge(sem("p0_done"), b * NTRIO + t + 1)
                    pool.sem_inc(passed, 1)
                    pool.tensor_copy(YB[:, :, :], Y[:, bass.ds(t * L, L), 0:C]).then_inc(sem("p0_y"), 1)
                barrier(pool, BASE0 + 4 + 3 * b)

            ones(ATT1, BASE1 + 1)
            with pool.Fori(0, B) as b:
                pool_rstd(pool, "ln1", b, NT, LN_EPS)
                pool_rstd(pool, "rms", b, NT, 1e-6)
                with pool.Fori(0, NTRIO) as t:
                    pool_slots(pool, ATT1, b * NTRIO + t)
                for i in range(2):
                    barrier(pool, BASE1 + 2 + 3 * b + i)
                with pool.Fori(0, NTRIO) as t:
                    pool_rstd(pool, "rm1", b * NTRIO + t, L, 1e-6)
                barrier(pool, BASE1 + 4 + 3 * b)
            pool.sem_inc(sem("table_free"), 1)
            ones(ATT2, BASE2 + 1)
            with pool.Fori(0, B) as b:
                pool_rstd(pool, "ln2", b, NT, LN_EPS)
                with pool.Fori(0, NTRIO) as t:
                    pool_slots(pool, ATT2, b * NTRIO + t)
                for i in range(3):
                    barrier(pool, BASE2 + 2 + 3 * b + i)
            ones(ATT3, BASE3 + 1)
            with pool.Fori(0, B) as b:
                pool_rstd(pool, "ln3", b, NT, LN_EPS)
            barrier(pool, BASE3 + 2)
            with pool.Fori(0, B) as b:
                with pool.Fori(0, 4) as n:
                    with pool.Fori(0, NTRIO) as t:
                        it = (b * 4 + n) * NTRIO + t
                        pool.wait_ge(sem("a3_stage_free"), it + 1)
                        pool.sem_inc(passed, 1)
                        pool.tensor_copy(STG[:, :, 0:D], SX[:, bass.ds(b * NT + t * L, L), bass.ds(n * D, D)])\
                            .then_inc(s(ATT3, "stage"), 1)
                        pool_slots(pool, ATT3, it)
                    for i in range(2):
                        barrier(pool, BASE3 + 3 + MEET3 * b + 2 * n + i)
                with pool.Fori(0, NTRIO) as t:
                    for i in range(2):
                        pool_rstd(pool, "n16", (b * NTRIO + t) * 2 + i, L * 4, 1e-8)
                barrier(pool, BASE3 + 3 + MEET3 * b + 8)

        @block.tensor
        def _(pe):
            pe.wait_ge(sem("weights_in"), 16)
            pe.sem_inc(passed, 1)
            for b in range(B):
                pe.wait_ge(sem("image_in"), 16 * B)
                pe.sem_inc(passed, 1)
                if b:
                    pe.wait_ge(sem("dyn"), b)
                    pe.sem_inc(passed, 1)
                for k in range(8):
                    mm = pe.matmul(PS[0:16, k, :], wt("conv1", C), XC[:, b, k * 512:(k + 1) * 512], start=True, stop=True)
                mm.then_inc(sem("conv1"), 1)
                pe.wait_ge(sem("relu"), b + 1)
                pe.sem_inc(passed, 1)
                for k in range(8):
                    mm = pe.matmul(PS[0:9, k, :], wt("conv2", 17), YC[:, k * 512:(k + 1) * 512], start=True, stop=True)
                mm.then_inc(sem("conv2"), 1)
            barrier(pe, 1)
            barrier(pe, 2)

            def transpose3(src, what, it, ident=identf, width=C):
                pe.wait_ge(sem(what + "_in"), it + 1)
                pe.sem_inc(passed, 1)
                for l in range(L):
                    o = PS[0:width, 0, l * P:(l + 1) * P] if ident is identf else PSH[0:width, l * P:(l + 1) * P]
                    mm = pe.transpose(o, src[:, l, 0:width], ident[:, :])
                mm.then_inc(sem(what + "_t"), 1)

            def project3(what, it, k, w, n, src=None):
                pe.wait_ge(sem(what + "_ts"), it + 1)
                pe.sem_inc(passed, 1)
                x_ = XT if src is None else src
                for l in range(L):
                    mm = pe.matmul(PS[:, 1 + l, 0:n], x_[0:k, l * P:(l + 1) * P], w, start=True, stop=True)
                mm.then_inc(sem(what + "_p"), 1)

            barrier(pe, BASE0 + 1)
            with pe.Fori(0, B) as b:
                with pe.Fori(0, NTRIO) as t:
                    it = b * NTRIO + t
                    transpose3(STG, "a0", it)
                    project3("a0", it, C + 1, wt("wqkv0", C + 1), 192)
                    pe_turn(pe, ATT0, it)
                barrier(pe, BASE0 + 2 + 3 * b)
                heads(pe, ATT0, lambda kvh, rr: pe_head(pe, ATT0, b, kvh, rr))
                barrier(pe, BASE0 + 3 + 3 * b)
                with pe.Fori(0, NTRIO) as t:
                    it = b * NTRIO + t
                    pe.wait_ge(sem("p0_y"), it + 1)
                    pe.sem_inc(passed, 1)
                    for l in range(L):
                        mm = pe.transpose(PSH[0:C, l * P:(l + 1) * P], YB[:, l, :], identh[:, :])
                    mm.then_inc(sem("p0_t"), 1)
                    project3("p0", it, C + 1, wt("wo0", C + 1), C)
                barrier(pe, BASE0 + 4 + 3 * b)

            barrier(pe, BASE1 + 1)
            with pe.Fori(0, B) as b:
                with pe.Fori(0, NTRIO) as t:
                    it = b * NTRIO + t
                    transpose3(STG, "a1", it)
                    project3("a1", it, C, wt("wqkv1", C), 128)
                    pe_turn(pe, ATT1, it)
                barrier(pe, BASE1 + 2 + 3 * b)
                heads(pe, ATT1, lambda kvh, rr: pe_head(pe, ATT1, b, kvh, rr))
                barrier(pe, BASE1 + 3 + 3 * b)
                with pe.Fori(0, NTRIO) as t:
                    it = b * NTRIO + t
                    transpose3(STG, "p1", it)
                    project3("p1", it, C, wt("wo1", C), C)
                    transpose3(OM, "m", it)
                    project3("m", it, C, wt("router", C), NE)
                    pe.wait_ge(sem("m_router_read"), it + 1)
                    pe.sem_inc(passed, 1)
                    for e in range(NE + 1):
                        if e < NE:
                            for hf in range(2):
                                i = 2 * e + hf
                                pe.wait_ge(sem("m_g"), it * 16 + i + 1)
                                pe.sem_inc(passed, 1)
                                for k, name in enumerate(("w1", "w3")):
                                    mm = pe.matmul(PS[0:HH, 2 * (i % 3) + k, 0:W3],
                                                   wt(name, C, e * HID + hf * HH, HH), XT[0:C, :],
                                                   start=True, stop=True)
                                mm.then_inc(sem("m_ab"), 1)
                        if e > 0:
                            f = e - 1
                            pe.wait_ge(sem("m_g"), it * 16 + 2 * f + 2 + 3)
                            pe.sem_inc(passed, 1)
                            pe.wait_ge(sem("m_acc"), it * NE + f + 1)
                            pe.sem_inc(passed, 1)
                            for l in range(L):
                                for hf in range(2):
                                    mm = pe.matmul(PS[:, 6 + f % 2, l * C:(l + 1) * C],
                                                   G[:, f % 2, hf, l * P:(l + 1) * P],
                                                   wt("w2", HH, (hf * NE + f) * C, C), start=hf == 0, stop=hf == 1)
                            mm.then_inc(sem("m_o"), 1)
                barrier(pe, BASE1 + 4 + 3 * b)
            barrier(pe, BASE2 + 1)
            with pe.Fori(0, B) as b:
                with pe.Fori(0, NTRIO) as t:
                    it = b * NTRIO + t
                    transpose3(STG, "a2", it)
                    pe.wait_ge(sem("a2_ts"), it + 1)
                    pe.sem_inc(passed, 1)
                    pe.matmul(PS[:, 1, 0:W3], wt("wcomp", C), XT[0:C, :], start=True, stop=True)\
                      .then_inc(sem("a2_c"), 1)
                    project3("a2c", it, P, wt("wsec", P), 192, CT)
                    pe_turn(pe, ATT2, it)
                barrier(pe, BASE2 + 2 + 3 * b)
                heads(pe, ATT2, lambda kvh, rr: pe_head(pe, ATT2, b, kvh, rr))
                barrier(pe, BASE2 + 3 + 3 * b)
                barrier(pe, BASE2 + 4 + 3 * b)
            barrier(pe, BASE3 + 1)
            with pe.Fori(0, B) as b:
                with pe.Fori(0, NTRIO) as t:
                    it = b * NTRIO + t
                    transpose3(STG, "sx", it)
                    project3("sx", it, C + 1, wt("hl", C + 1), C)
            barrier(pe, BASE3 + 2)
            with pe.Fori(0, B) as b:
                with pe.Fori(0, 4) as n:
                    with pe.Fori(0, NTRIO) as t:
                        it = (b * 4 + n) * NTRIO + t
                        pe.wait_ge(s(ATT3, "stage"), it + 1)
                        pe.sem_inc(passed, 1)
                        for l in range(L):
                            mm = pe.transpose(PS[0:D, 0, l * P:(l + 1) * P], STG[:, l, 0:D], identf[:, :])
                        mm.then_inc(sem("a3_t"), 1)
                        pe.wait_ge(sem("a3_ts"), it + 1)
                        pe.sem_inc(passed, 1)
                        at = COLS["wn"][0]
                        for l in range(L):
                            mm = pe.matmul(PS[:, 1 + l, 0:96], XT[0:D, l * P:(l + 1) * P],
                                           WP[0:D, bass.ds(n * 96 + at, 96)], start=True, stop=True)
                        mm.then_inc(sem("a3_p"), 1)
                        pe_turn(pe, ATT3, it)
                    barrier(pe, BASE3 + 3 + MEET3 * b + 2 * n)
                    heads(pe, ATT3, lambda kvh, rr: pe_head(pe, ATT3, b * 4 + n, kvh, rr))
                    barrier(pe, BASE3 + 4 + MEET3 * b + 2 * n)
                with pe.Fori(0, NTRIO) as t:
                    it = b * NTRIO + t
                    pe.wait_ge(sem("p3_om"), it + 1)
                    pe.sem_inc(passed, 1)
                    for hp in range(2):
                        for l in range(L):
                            mm = pe.transpose(PS[:, hp, l * P:(l + 1) * P], OM[:, l, hp * P:(hp + 1) * P], identf[:, :])
                    mm.then_inc(sem("p3_omt"), 1)
                    pe.wait_ge(sem("p3_ot"), it + 1)
                    pe.sem_inc(passed, 1)
                    for l in range(L):
                        for hp in range(2):
                            mm = pe.matmul(PS[:, 2, (2 * l + hp) * 8:(2 * l + hp + 1) * 8], OT[:, hp, l * P:(l + 1) * P],
                                           wt("gate", P, hp * 8, 8), start=True, stop=True)
                    mm.then_inc(sem("p3_gate"), 1)
                    for i, (w, k, n_) in enumerate((("fc1", C + 1, C), ("fc2", C + 1, C), ("fgate", C, 4))):
                        transpose3(STG, "p3", it * 3 + i)
                        project3("p3", it * 3 + i, k, wt(w, k), n_)
                barrier(pe, BASE3 + 3 + MEET3 * b + 8)

        @block.scalar
        def _(act):
            act.preload_act_table(ACT.Exp)
            act.wait_ge(sem("weights_in"), 16)
            act.sem_inc(passed, 1)
            act.wait_ge(sem("ones_row"), 1)
            act.sem_inc(passed, 1)
            act.wait_ge(sem("bn_ready"), 1)
            act.sem_inc(passed, 1)
            for b in range(B):
                act.wait_ge(sem("conv1"), b + 1)
                act.sem_inc(passed, 1)
                for k in range(8):
                    last = act.activation(YC[0:16, k * 512:(k + 1) * 512], PS[0:16, k, :], ACT.Relu,
                                          bias=bnv[:, 3:4], scale=bnv[:, 1:2])
                last.then_inc(sem("relu"), 1)
                act.wait_ge(sem("conv2"), b + 1)
                act.sem_inc(passed, 1)
                if b:
                    act.wait_ge(sem("dyn_out"), 16 * b)
                    act.sem_inc(passed, 1)
                for k in range(8):
                    last = act.activation(WD[:, k * 512:(k + 1) * 512], PS[0:9, k, :], ACT.Copy)
                last.then_inc(sem("dyn"), 1)
            barrier(act, 1)
            barrier(act, 2)

            def take_t(what, it, scale=None):
                act.wait_ge(sem(what + "_t"), it + 1)
                act.sem_inc(passed, 1)
                if scale is None:
                    act.activation(XT[0:C, :], PS[0:C, 0, 0:W3], ACT.Copy).then_inc(sem(what + "_ts"), 1)
                else:
                    act.activation(XT[0:C, :], PS[0:C, 0, 0:W3], ACT.Identity, scale=scale)\
                       .then_inc(sem(what + "_ts"), 1)

            def take_q(lay, what, it):
                act.wait_ge(sem(what + "_p"), it + 1)
                act.sem_inc(passed, 1)
                act.activation(QK[:, :, 0:lay.nq], PS[:, 1:1 + L, 0:lay.nq], ACT.Copy, scale=lay.qscale)
                act.activation(QK[:, :, lay.nq:lay.nq + lay.nk], PS[:, 1:1 + L, lay.nq:lay.nq + lay.nk], ACT.Copy)\
                   .then_inc(s(lay, "q"), 1)

            barrier(act, BASE0 + 1)
            with act.Fori(0, B) as b:
                with act.Fori(0, NTRIO) as t:
                    it = b * NTRIO + t
                    take_t("a0", it)
                    take_q(ATT0, "a0", it)
                    put_values(act, ATT0, t, 128)
                    put_turned(act, ATT0, it, t, 0)
                barrier(act, BASE0 + 2 + 3 * b)
                heads(act, ATT0, lambda kvh, rr: act_head(act, ATT0, b, kvh, rr))
                barrier(act, BASE0 + 3 + 3 * b)
                with act.Fori(0, NTRIO) as t:
                    it = b * NTRIO + t
                    act.wait_ge(sem("p0_t"), it + 1)
                    act.sem_inc(passed, 1)
                    act.activation(XT[0:C, :], PSH[0:C, 0:W3], ACT.Copy).then_inc(sem("p0_ts"), 1)
                barrier(act, BASE0 + 4 + 3 * b)
            barrier(act, BASE1 + 1)
            with act.Fori(0, B) as b:
                with act.Fori(0, NTRIO) as t:
                    it = b * NTRIO + t
                    take_t("a1", it, wt("ln1", C))
                    take_q(ATT1, "a1", it)
                    put_values(act, ATT1, t, 96)
                    put_turned(act, ATT1, it, t, 0)
                barrier(act, BASE1 + 2 + 3 * b)
                heads(act, ATT1, lambda kvh, rr: act_head(act, ATT1, b, kvh, rr))
                barrier(act, BASE1 + 3 + 3 * b)
                with act.Fori(0, NTRIO) as t:
                    it = b * NTRIO + t
                    take_t("p1", it)
                    take_t("m", it, wt("ln2", C))
                    act.wait_ge(sem("m_logit"), it + 1)
                    act.sem_inc(passed, 1)
                    act.activation(S1[:, 1, 0:L * NE], S1[:, 0, 0:L * NE], ACT.Exp).then_inc(sem("m_exp"), 1)
                    for i in range(2 * NE):
                        act.wait_ge(sem("m_ab"), it * 16 + i + 1)
                        act.sem_inc(passed, 1)
                        act.wait_ge(sem("m_g"), it * 16 + i + 1)
                        act.sem_inc(passed, 1)
                        act.activation(E1[0:HH, 2 * (i % 3):2 * (i % 3) + 2, :].rearrange("p a b -> p (a b)"),
                                       PS[0:HH, 2 * (i % 3), 0:W3], ACT.Tanh, scale=0.5).then_inc(sem("m_s"), 1)
                barrier(act, BASE1 + 4 + 3 * b)
            barrier(act, BASE2 + 1)
            with act.Fori(0, B) as b:
                with act.Fori(0, NTRIO) as t:
                    it = b * NTRIO + t
                    take_t("a2", it)
                    act.wait_ge(sem("a2_c"), it + 1)
                    act.sem_inc(passed, 1)
                    act.activation(CT[:, :], PS[:, 1, 0:W3], ACT.Copy).then_inc(sem("a2c_ts"), 1)
                    take_q(ATT2, "a2c", it)
                    put_values(act, ATT2, t, 128)
                    put_turned(act, ATT2, it, t, 0)
                barrier(act, BASE2 + 2 + 3 * b)
                heads(act, ATT2, lambda kvh, rr: act_head(act, ATT2, b, kvh, rr))
                barrier(act, BASE2 + 3 + 3 * b)
                barrier(act, BASE2 + 4 + 3 * b)
            barrier(act, BASE3 + 1)
            with act.Fori(0, B) as b:
                with act.Fori(0, NTRIO) as t:
                    it = b * NTRIO + t
                    take_t("sx", it)
            barrier(act, BASE3 + 2)
            with act.Fori(0, B) as b:
                with act.Fori(0, 4) as n:
                    with act.Fori(0, NTRIO) as t:
                        it = (b * 4 + n) * NTRIO + t
                        act.wait_ge(sem("a3_t"), it + 1)
                        act.sem_inc(passed, 1)
                        act.activation(XT[0:D, :], PS[0:D, 0, 0:W3], ACT.Copy).then_inc(sem("a3_ts"), 1)
                        take_q(ATT3, "a3", it)
                        put_values(act, ATT3, t, 80)
                        put_turned(act, ATT3, it, t, 0)
                    barrier(act, BASE3 + 3 + MEET3 * b + 2 * n)
                    heads(act, ATT3, lambda kvh, rr: act_head(act, ATT3, b * 4 + n, kvh, rr))
                    barrier(act, BASE3 + 4 + MEET3 * b + 2 * n)
                with act.Fori(0, NTRIO) as t:
                    it = b * NTRIO + t
                    act.wait_ge(sem("p3_omt"), it + 1)
                    act.sem_inc(passed, 1)
                    act.activation(OT[:, :, :], PS[:, 0:2, 0:W3], ACT.Copy).then_inc(sem("p3_ot"), 1)
                    act.wait_ge(sem("p3_logit"), it * 2 + 1)
                    act.sem_inc(passed, 1)
                    act.activation(S1[:, 1, :], S1[:, 0, :], ACT.Exp).then_inc(sem("p3_exp"), 1)
                    for i in range(3):
                        take_t("p3", it * 3 + i)
                    act.wait_ge(sem("p3_logit"), it * 2 + 2)
                    act.sem_inc(passed, 1)
                    act.activation(S1[:, 1, 0:L * 4], S1[:, 0, 0:L * 4], ACT.Exp).then_inc(sem("p3_exp"), 1)
                barrier(act, BASE3 + 3 + MEET3 * b + 8)

        @block.vector
        def _(dve):
            dve.wait_ge(sem("weights_in"), 16)
            dve.sem_inc(passed, 1)
            at = COLS["bn"][0]
            b1, mean, gamma, var, beta = (WP[0:16, at + i:at + i + 1] for i in range(5))
            dve.wait_ge(sem("bn_rstd"), 1)
            dve.sem_inc(passed, 1)
            dve.tensor_tensor(bnv[:, 1:2], bnv[:, 2:3], gamma, ALU.mult)
            dve.tensor_tensor(bnv[:, 0:1], b1, mean, ALU.subtract)
            dve.drain()
            dve.tensor_tensor(bnv[:, 2:3], bnv[:, 0:1], bnv[:, 1:2], ALU.mult)
            dve.drain()
            dve.tensor_tensor(bnv[:, 3:4], bnv[:, 2:3], beta, ALU.add).then_inc(sem("bn_ready"), 1)
            for b in range(B):
                dve.wait_ge(sem("shift_in"), 16 * 24 * (b + 1))
                dve.sem_inc(passed, 1)
                dve.wait_ge(sem("rows_in"), 16 * 2 * (b + 1))
                dve.sem_inc(passed, 1)
                hb = H[:, b * NT:b * NT + 32, :]
                for k in range(9):
                    i, j = divmod(k, 3)
                    w = WB[:, k, :].unsqueeze(1).broadcast_to([P, 32, IMG])
                    dve.tensor_tensor(hb if k == 0 else TM[:, k % 2], XS[:, i, :, j:j + IMG], w, ALU.mult)
                    dve.drain()
                    if k:
                        dve.tensor_tensor(hb, hb, TM[:, k % 2], ALU.add)
                dve.drain()
                dve.sem_inc(sem("shift_free"), 1)
            barrier(dve, 1)
            for lay in (ATT0, ATT1, ATT2, ATT3):
                dve.sem_inc(s(lay, "maxbank_free"), L)
                dve.sem_inc(s(lay, "exps"), L)
                dve.sem_inc(s(lay, "values"), L)
                dve.sem_inc(s(lay, "out_free"), 1)
            dve.sem_inc(sem("p0_done"), 1)
            dve.sem_inc(sem("a3_stage_free"), 1)
            dve.sem_inc(sem("m_g"), 3)
            dve.sem_inc(sem("m_acc"), 2)
            dve.wait_ge(sem("text_in"), 16 * B)
            dve.sem_inc(passed, 1)
            barrier(dve, 2)

            def take_k(lay, it):
                dve.wait_ge(s(lay, "q"), it + 1)
                dve.sem_inc(passed, 1)

            barrier(dve, BASE0 + 1)
            with dve.Fori(0, B) as b:
                dve_layernorm(dve, b, "ln0", SX[:, 0:NT, :])
                with dve.Fori(0, NTRIO) as t:
                    it = b * NTRIO + t
                    dve.tensor_scalar(STG[:, :, :], XN[:, bass.ds(t * L, L), :], -10000.0, 10000.0, ALU.max, ALU.min)\
                       .then_inc(sem("a0_in"), 1)
                    take_k(ATT0, it)
                    dve_split(dve, ATT0, it)
                    put_turned(dve, ATT0, it, t, 1)
                    dve.wait_ge(s(ATT0, "put"), 2 * it + 2)
                    dve.sem_inc(passed, 1)
                    dve.sem_inc(passed, 1)
                barrier(dve, BASE0 + 2 + 3 * b)
                heads(dve, ATT0, lambda kvh, rr: dve_head(dve, ATT0, b, kvh, rr, kvh * ATT0.rep + rr))
                barrier(dve, BASE0 + 3 + 3 * b)
                with dve.Fori(0, NTRIO) as t:
                    it = b * NTRIO + t
                    dve.wait_ge(sem("p0_p"), it + 1)
                    dve.sem_inc(passed, 1)
                    hb = H[:, bass.ds(b * NT + t * L, L), :]
                    dve.tensor_tensor(hb, hb, PS[:, 1:1 + L, 0:C], ALU.add).then_inc(sem("p0_done"), 1)
                barrier(dve, BASE0 + 4 + 3 * b)

            def softmax(src, n, k, what, it):
                m = S1[:, 3, 0:n]
                lo = S1[:, 0, 0:n * k].rearrange("p (a b) -> p a b", b=k)
                ex = S1[:, 1, 0:n * k].rearrange("p (a b) -> p a b", b=k)
                pr = S1[:, 2, 0:n * k].rearrange("p (a b) -> p a b", b=k)
                dve.tensor_reduce(m, src, AX, ALU.max, negate=True)
                dve.drain()
                dve.tensor_tensor(lo, src, m.unsqueeze(2).broadcast_to([P, n, k]), ALU.add)\
                   .then_inc(sem(what + "_logit"), 1)
                dve.wait_ge(sem(what + "_exp"), it + 1)
                dve.sem_inc(passed, 1)
                dve.tensor_reduce(S1[:, 4, 0:n], ex, AX, ALU.add)
                dve.drain()
                dve.reciprocal(m, S1[:, 4, 0:n])
                dve.drain()
                dve.tensor_tensor(pr, ex, m.unsqueeze(2).broadcast_to([P, n, k]), ALU.mult)
                dve.drain()
                return pr

            def rms(dst, src, n, what, k):
                sq = SX[:, 0:n, :]
                dve.tensor_tensor(sq, src, src, ALU.mult)
                dve.drain()
                dve.tensor_reduce(st[:, 2, 0:n], sq, AX, ALU.add)
                dve.drain()
                dve.tensor_scalar(st[:, 3, 0:n], st[:, 2, 0:n], 1.0 / C, None, ALU.mult)
                ask_rstd(dve, what, k)
                return dve.tensor_tensor(dst, src, st[:, 2, 0:n].unsqueeze(2).broadcast_to([P, n, C]), ALU.mult)

            dve.wait_ge(sem("table_in"), 16)
            dve.sem_inc(passed, 1)
            before = E1[:, 6, 0:64].rearrange("p (a b) -> p a b", b=NE)
            for e in range(NE):
                dve.memset(before[:, e, :], 0.0)
                if e:
                    dve.drain()
                    dve.memset(before[:, e, 0:e], 1.0)
            barrier(dve, BASE1 + 1)
            with dve.Fori(0, B) as b:
                dve_layernorm(dve, b, "ln1", SX[:, 0:NT, :])
                sq = SX[:, 0:NT, :]
                xr_ = SX[:, NT:2 * NT, :]
                rms(xr_, XN[:, :, :], NT, "rms", b)
                dve.drain()
                with dve.Fori(0, NTRIO) as t:
                    it = b * NTRIO + t
                    dve.tensor_copy(STG[:, :, :], SX[:, bass.ds(t * L + NT, L), :]).then_inc(sem("a1_in"), 1)
                    n = ATT1.nq + ATT1.nk
                    nh = n // D
                    take_k(ATT1, it)
                    for l in range(L):
                        cos = RT[:, 0, bass.ds(t * L + l, 1), :].broadcast_to([P, nh, D])
                        sin = RT[:, 1, bass.ds(t * L + l, 1), :].broadcast_to([P, nh, D])
                        q = QK[:, l, 0:n].rearrange("p (h d) -> p h d", d=D)
                        r1 = R1[:, l, 0:n].rearrange("p (h d) -> p h d", d=D)
                        r2 = R2[:, l, 0:n].rearrange("p (h d) -> p h d", d=D)
                        dve.tensor_tensor(r1, q, cos, ALU.mult)
                        dve.tensor_tensor(r2[:, :, 0:D // 2], q[:, :, D // 2:D], sin[:, :, 0:D // 2], ALU.mult)
                        dve.tensor_tensor(r2[:, :, D // 2:D], q[:, :, 0:D // 2], sin[:, :, D // 2:D], ALU.mult)
                    dve.drain()
                    dve.tensor_tensor(QK[:, :, 0:n], R1[:, :, 0:n], R2[:, :, 0:n], ALU.add)
                    dve.drain()
                    dve_split(dve, ATT1, it)
                    put_turned(dve, ATT1, it, t, 1)
                    dve.wait_ge(s(ATT1, "put"), 2 * it + 2)
                    dve.sem_inc(passed, 1)
                    dve.sem_inc(passed, 1)
                barrier(dve, BASE1 + 2 + 3 * b)
                heads(dve, ATT1, lambda kvh, rr: dve_head(dve, ATT1, b, kvh, rr, kvh * ATT1.rep + rr))
                barrier(dve, BASE1 + 3 + 3 * b)
                with dve.Fori(0, NTRIO) as t:
                    it = b * NTRIO + t
                    dve.tensor_copy(STG[:, :, :], Y[:, bass.ds(t * L, L), 0:C]).then_inc(sem("p1_in"), 1)
                    dve.wait_ge(sem("p1_p"), it + 1)
                    dve.sem_inc(passed, 1)
                    dve.tensor_tensor(X1[:, :, :], XN[:, bass.ds(t * L, L), :], PS[:, 1:1 + L, 0:C], ALU.add)
                    dve.drain()
                    rms(OM[:, :, 0:C], X1[:, :, :], L, "rm1", it).then_inc(sem("m_in"), 1)
                    dve.wait_ge(sem("m_p"), it + 1)
                    dve.sem_inc(passed, 1)
                    pr = softmax(PS[:, 1:1 + L, 0:NE], L, NE, "m", it)
                    dve.sem_inc(sem("m_router_read"), 1)
                    gt = E1[:, 6, 64:128].rearrange("p (a b) -> p a b", b=NE)
                    eq = E1[:, 6, 128:192].rearrange("p (a b) -> p a b", b=NE)
                    rank = S1[:, 5, 0:L * NE].rearrange("p (a b) -> p a b", b=NE)
                    for l in range(L):
                        mine = pr[:, l, :].unsqueeze(2).broadcast_to([P, NE, NE])
                        other = pr[:, l, :].unsqueeze(1).broadcast_to([P, NE, NE])
                        dve.tensor_tensor(gt, other, mine, ALU.is_gt)
                        dve.tensor_tensor(eq, other, mine, ALU.is_equal)
                        dve.drain()
                        dve.tensor_tensor(eq, eq, before, ALU.mult)
                        dve.drain()
                        dve.tensor_tensor(gt, gt, eq, ALU.add)
                        dve.drain()
                        dve.tensor_reduce(rank[:, l, :], gt, AX, ALU.add)
                        dve.drain()
                    sel = S1[:, 6, 0:L * NE].rearrange("p (a b) -> p a b", b=NE)
                    dve.tensor_scalar(sel, rank, 1.5, None, ALU.is_lt)
                    dve.drain()
                    dve.tensor_tensor(rank, sel, pr, ALU.mult)
                    dve.drain()
                    dve.tensor_reduce(S1[:, 4, 0:L], rank, AX, ALU.add)
                    dve.drain()
                    dve.tensor_scalar(S1[:, 3, 0:L], S1[:, 4, 0:L], 1e-9, None, ALU.add)
                    dve.drain()
                    dve.reciprocal(S1[:, 4, 0:L], S1[:, 3, 0:L])
                    dve.drain()
                    dve.tensor_scalar(S1[:, 3, 0:L], S1[:, 4, 0:L], 0.5, None, ALU.mult)
                    dve.drain()
                    dve.tensor_tensor(sel, rank, S1[:, 3, 0:L].unsqueeze(2).broadcast_to([P, L, NE]), ALU.mult)
                    dve.drain()

                    def add_expert(f):
                        dve.wait_ge(sem("m_o"), it * NE + f + 1)
                        dve.sem_inc(passed, 1)
                        tmp = STG[:, :, :]
                        dve.tensor_tensor(tmp, PS[:, 6 + f % 2, 0:L * C].rearrange("p (l c) -> p l c", c=C),
                                          sel[:, :, f].unsqueeze(2).broadcast_to([P, L, C]), ALU.mult)\
                           .then_inc(sem("m_acc"), 1)
                        dve.drain()
                        dve.tensor_tensor(X1[:, :, :], X1[:, :, :], tmp, ALU.add)
                        dve.drain()

                    for i in range(2 * NE):
                        e, hf = divmod(i, 2)
                        dve.wait_ge(sem("m_s"), it * 16 + i + 1)
                        dve.sem_inc(passed, 1)
                        th = E1[0:HH, 2 * (i % 3):2 * (i % 3) + 2, :].rearrange("p a b -> p (a b)")
                        ra = (R1, R2)[i % 2][0:HH, :, :].rearrange("p a b -> p (a b)")
                        dve.scalar_tensor_tensor(out=ra, in0=th, scalar=1.0,
                                                 in1=PS[0:HH, 2 * (i % 3), 0:W3], op0=ALU.add, op1=ALU.mult)
                        dve.drain()
                        dve.tensor_tensor(G[:, e % 2, hf, :], ra,
                                          PS[0:HH, 2 * (i % 3) + 1, 0:W3], ALU.mult).then_inc(sem("m_g"), 1)
                        if hf and e >= 1:
                            add_expert(e - 1)
                    add_expert(NE - 1)
                    hb = H[:, bass.ds(b * NT + t * L, L), :]
                    dve.tensor_tensor(hb, hb, X1[:, :, :], ALU.add)
                    dve.drain()
                barrier(dve, BASE1 + 4 + 3 * b)
            dve.wait_ge(sem("table_in"), 32)
            dve.sem_inc(passed, 1)
            barrier(dve, BASE2 + 1)
            with dve.Fori(0, B) as b:
                dve_layernorm(dve, b, "ln2", SX[:, 0:NT, :])
                with dve.Fori(0, NTRIO) as t:
                    it = b * NTRIO + t
                    dve.tensor_copy(STG[:, :, :], XN[:, bass.ds(t * L, L), :]).then_inc(sem("a2_in"), 1)
                    take_k(ATT2, it)
                    for half in range(2):
                        q = QK[:, :, half * C + 48:half * C + 64].rearrange("p l (i two) -> p l i two", two=2)
                        q1, q2 = q[:, :, :, 0], q[:, :, :, 1]
                        cos = RT[:, 0, bass.ds(t * L, L), 0:D // 2]
                        sin = RT[:, 1, bass.ds(t * L, L), 0:D // 2]
                        r = [R2[:, :, i * 8:(i + 1) * 8] for i in range(4)]
                        dve.tensor_tensor(r[0], q1, cos, ALU.mult)
                        dve.tensor_tensor(r[1], q2, sin, ALU.mult)
                        dve.tensor_tensor(r[2], q1, sin, ALU.mult)
                        dve.tensor_tensor(r[3], q2, cos, ALU.mult)
                        dve.drain()
                        dve.tensor_tensor(q1, r[0], r[1], ALU.subtract)
                        dve.tensor_tensor(q2, r[2], r[3], ALU.add)
                        dve.drain()
                    dve_split(dve, ATT2, it)
                    put_turned(dve, ATT2, it, t, 1)
                    dve.wait_ge(s(ATT2, "put"), 2 * it + 2)
                    dve.sem_inc(passed, 1)
                    dve.sem_inc(passed, 1)
                barrier(dve, BASE2 + 2 + 3 * b)
                heads(dve, ATT2, lambda kvh, rr: dve_head(dve, ATT2, b, kvh, rr, 0))
                barrier(dve, BASE2 + 3 + 3 * b)
                hb = H[:, bass.ds(b * NT, NT), :]
                dve.tensor_tensor(hb, hb, Y[:, :, 0:C], ALU.add)
                barrier(dve, BASE2 + 4 + 3 * b)
            barrier(dve, BASE3 + 1)
            with dve.Fori(0, B) as b:
                dve_layernorm(dve, b, "ln3", Y[:, :, 0:C])
                with dve.Fori(0, NTRIO) as t:
                    it = b * NTRIO + t
                    dve.tensor_copy(STG[:, :, :], XN[:, bass.ds(t * L, L), :]).then_inc(sem("sx_in"), 1)
                    dve.wait_ge(sem("sx_p"), it + 1)
                    dve.sem_inc(passed, 1)
                    dve.tensor_copy(SX[:, bass.ds(b * NT + t * L, L), :], PS[:, 1:1 + L, 0:C])
                    dve.drain()
            barrier(dve, BASE3 + 2)
            g4 = L * 4

            def norm16(dst, src, g, b_, k):
                mu, sq = S1[:, 3, 0:g4], E1[:, 7, 0:L * C].rearrange("p (a b) -> p a b", b=D)
                var, mean, rstd = S1[:, 4, 0:g4], st[:, 3, 0:g4], st[:, 2, 0:g4]
                xc = E1[:, 6, 0:L * C].rearrange("p (a b) -> p a b", b=D)
                dve.tensor_reduce(var, src, AX, ALU.add)
                dve.drain()
                dve.tensor_scalar(mu, var, 1.0 / D, None, ALU.mult)
                dve.drain()
                dve.tensor_tensor(xc, src, mu.unsqueeze(2).broadcast_to([P, g4, D]), ALU.subtract)
                dve.drain()
                dve.tensor_tensor(sq, xc, xc, ALU.mult)
                dve.drain()
                dve.tensor_reduce(var, sq, AX, ALU.add)
                dve.drain()
                dve.tensor_scalar(mean, var, 1.0 / D, None, ALU.mult)
                ask_rstd(dve, "n16", k)
                dve.tensor_tensor(sq, xc, rstd.unsqueeze(2).broadcast_to([P, g4, D]), ALU.mult)
                dve.drain()
                dve.tensor_tensor(xc, sq, wt(g, P).unsqueeze(1).broadcast_to([P, g4, D]), ALU.mult)
                dve.drain()
                return dve.tensor_tensor(dst, xc, wt(b_, P).unsqueeze(1).broadcast_to([P, g4, D]), ALU.add)

            def by16(ap):
                return ap.rearrange("p l (n d) -> p (l n) d", d=D)

            with dve.Fori(0, B) as b:
                with dve.Fori(0, 4) as n:
                    with dve.Fori(0, NTRIO) as t:
                        it = (b * 4 + n) * NTRIO + t
                        take_k(ATT3, it)
                        dve_split(dve, ATT3, it)
                        put_turned(dve, ATT3, it, t, 1)
                        dve.wait_ge(s(ATT3, "put"), 2 * it + 2)
                        dve.sem_inc(passed, 1)
                        dve.sem_inc(sem("a3_stage_free"), 1)
                    barrier(dve, BASE3 + 3 + MEET3 * b + 2 * n)
                    heads(dve, ATT3, lambda kvh, rr: dve_head(dve, ATT3, b * 4 + n, kvh, rr, n * 4 + rr))
                    barrier(dve, BASE3 + 4 + MEET3 * b + 2 * n)
                with dve.Fori(0, NTRIO) as t:
                    it = b * NTRIO + t
                    nz = E1[:, 0, :].rearrange("p (l c) -> p l c", c=C)
                    dve.tensor_scalar(nz, SX[:, bass.ds(b * NT + t * L, L), :], 0.0, None, ALU.not_equal)
                    dve.drain()
                    for l in range(L):
                        dve.tensor_tensor(OM[:, l, :].rearrange("p (n e d) -> p n e d", e=4, d=D),
                                          Y[:, bass.ds(t * L + l, 1), :].rearrange("p a (n e d) -> p (a n) e d", e=4, d=D),
                                          nz[:, l, :].rearrange("p (n d) -> p n d", d=D).unsqueeze(2)
                                          .broadcast_to([P, 4, 4, D]), ALU.mult)
                    dve.drain()
                    dve.sem_inc(sem("p3_om"), 1)
                    dve.wait_ge(sem("p3_gate"), it + 1)
                    dve.sem_inc(passed, 1)
                    gl = E1[:, 1, 0:L * 16].rearrange("p (l c) -> p l c", c=16)
                    dve.tensor_tensor(gl, PS[:, 2, 0:L * 16].rearrange("p (l c) -> p l c", c=16),
                                      wt("gateb", P).unsqueeze(1).broadcast_to([P, L, 16]), ALU.add)
                    dve.drain()
                    gs = softmax(gl.rearrange("p l (n e) -> p (l n) e", e=4), g4, 4, "p3", it * 2)
                    for l in range(L):
                        om = OM[:, l, :].rearrange("p (n e d) -> p n e d", e=4, d=D)
                        dve.tensor_tensor(om, om, gs[:, 4 * l:4 * l + 4, :].unsqueeze(3).broadcast_to([P, 4, 4, D]),
                                          ALU.mult)
                    dve.drain()
                    m4 = OM[:, :, :].rearrange("p l (n e d) -> p (l n) (e d)", e=4, d=D)
                    half = E1[:, 2:4, :].rearrange("p a b -> p (a b)")[:, 0:g4 * 32].rearrange("p (a b) -> p a b", b=32)
                    dve.tensor_tensor(half, m4[:, :, 0:32], m4[:, :, 32:64], ALU.add)
                    dve.drain()
                    mix = by16(E1[:, 4, :].rearrange("p (l c) -> p l c", c=C))
                    dve.tensor_tensor(mix, half[:, :, 0:D], half[:, :, D:2 * D], ALU.add)
                    dve.drain()
                    mx = E1[:, 4, :].rearrange("p (l c) -> p l c", c=C)
                    dve.tensor_tensor(mx[:, :, 0:D], mx[:, :, 0:D], SX[:, bass.ds(t * L, L), 0:D], ALU.add)
                    dve.tensor_tensor(mx[:, :, D:C], mx[:, :, D:C], SX[:, bass.ds(t * L + NT, L), D:C], ALU.add)
                    dve.drain()
                    fx = X1[:, :, :]
                    norm16(by16(fx), mix, "lng", "lnb", it * 2)
                    dve.drain()
                    dve.tensor_scalar(nz, fx, 0.0, None, ALU.not_equal)
                    dve.tensor_copy(STG[:, :, :], fx).then_inc(sem("p3_in"), 1)
                    dve.wait_ge(sem("p3_p"), it * 3 + 1)
                    dve.sem_inc(passed, 1)
                    dve.scalar_tensor_tensor(out=STG[:, :, :], in0=PS[:, 1:1 + L, 0:C], scalar=0.0, in1=nz,
                                             op0=ALU.max, op1=ALU.mult).then_inc(sem("p3_in"), 1)
                    dve.wait_ge(sem("p3_p"), it * 3 + 2)
                    dve.sem_inc(passed, 1)
                    dve.tensor_tensor(mx, PS[:, 1:1 + L, 0:C], nz, ALU.mult)
                    dve.drain()
                    dve.tensor_tensor(nz, mx, fx, ALU.add)
                    dve.drain()
                    fo = E1[:, 5, :].rearrange("p (l c) -> p l c", c=C)
                    norm16(by16(fo), by16(nz), "fng", "fnb", it * 2 + 1)
                    dve.drain()
                    dve.tensor_copy(STG[:, :, :], fo).then_inc(sem("p3_in"), 1)
                    dve.wait_ge(sem("p3_p"), it * 3 + 3)
                    dve.sem_inc(passed, 1)
                    fg = softmax(PS[:, 1:1 + L, 0:4], L, 4, "p3", it * 2 + 1)
                    dve.tensor_tensor(by16(mx), by16(fo), fg.rearrange("p a b -> p (a b)").unsqueeze(2)
                                      .broadcast_to([P, g4, D]), ALU.mult)
                    dve.drain()
                    hb = H[:, bass.ds(b * NT + t * L, L), :]
                    dve.tensor_tensor(hb, hb, mx, ALU.add)
                    dve.drain()
                barrier(dve, BASE3 + 3 + MEET3 * b + 8)
            dve.sem_inc(sem("final"), 1)


def kernel(**inputs):
    import numpy as np
    import concourse.bacc as bacc
    from concourse import mybir as mb
    from concourse.bass_utils import run_bass_kernel_spmd as run

    a = {k: np.ascontiguousarray(v) for k, v in inputs.items()}
    wp = np.zeros((P, NCOLS), np.float32)

    def put(name, block, col=0, row=0):
        at = COLS[name][0] + col
        wp[row:row + block.shape[0], at:at + block.shape[1]] = block

    put("conv1", a["L0_tok_conv1_w"].T)
    for i, name in enumerate(("conv1_b", "bn_mean", "bn_gamma", "bn_var", "bn_beta")):
        put("bn", a["L0_tok_" + name][:, None], i)
    put("conv2", a["L0_tok_conv2_w"].T)
    put("conv2", a["L0_tok_conv2_b"][None, :], 0, 16)
    for i, name in enumerate("qkv"):
        put("wqkv0", a["L0_attn_W" + name].T, 64 * i)
        put("wqkv0", a["L0_attn_b" + name][None, :], 64 * i, 64)
    put("wo0", a["L0_attn_Wo"].T)
    put("wo0", a["L0_attn_bo"][None, :], 0, 64)
    put("ln1", a["L0_ffn_ln1_w"][:, None])
    put("ln2", a["L0_ffn_ln2_w"][:, None])
    put("wqkv1", a["L0_ffn_wq"].T, 0)
    put("wqkv1", a["L0_ffn_wk"].T, 64)
    put("wqkv1", a["L0_ffn_wv"].T, 96)
    put("wo1", a["L0_ffn_wo"].T)
    put("router", a["L0_ffn_router_w"].T)
    for e in range(NE):
        put("w1", a["L0_ffn_w1"][e].T, e * HID)
        put("w3", a["L0_ffn_w3"][e].T, e * HID)
        for hf in range(2):
            put("w2", a["L0_ffn_w2"][e].T[hf * HH:(hf + 1) * HH], (hf * NE + e) * C)
    put("wcomp", a["L1_attn_Wq_comp"], 0)
    put("wcomp", a["L1_attn_Wkv_comp"], 64)
    put("wsec", a["L1_attn_Wqc"], 0)
    put("wsec", a["L1_attn_Wqr"], 48)
    put("wsec", a["L1_attn_Wkc"], 64, 64)
    put("wsec", a["L1_attn_Wkr"], 112, 64)
    put("wsec", a["L1_attn_Wv"], 128, 64)
    put("hl", a["L1_ffn_hl_w"].reshape(64, 64).T)
    put("hl", a["L1_ffn_hl_b"].reshape(1, 64), 0, 64)
    for n in range(4):
        for e in range(4):
            put("wn", a["L1_ffn_wq"][n, e].T, n * 96 + e * D)
        put("wn", a["L1_ffn_wk"][n].T, n * 96 + 64)
        put("wn", a["L1_ffn_wv"][n].T, n * 96 + 80)
        put("gate", a["L1_ffn_gate_w"][n].T, n * 4, (n % 2) * 64)
        for name in ("fc1", "fc2"):
            put(name, a[f"L1_ffn_{name}_w"].T, n * D, n * D)
            put(name, a[f"L1_ffn_{name}_b"][None, :], n * D, 64)
    put("gateb", np.tile(a["L1_ffn_gate_b"].reshape(1, 16), (P, 1)))
    for col, name in (("lng", "ln_g"), ("lnb", "ln_b"), ("fng", "fnorm_g"), ("fnb", "fnorm_b")):
        put(col, np.tile(a["L1_ffn_" + name][None, :], (P, 1)))
    put("fgate", a["L1_ffn_fgate_w"].T)

    inv = 1.0 / 10000.0 ** (np.arange(0, D, 2, dtype=np.float32) / D)
    ang = np.outer(np.arange(T, dtype=np.float32), inv)
    cos = np.cos(np.concatenate([ang, ang], -1)).astype(np.float32)
    sin = np.sin(np.concatenate([ang, ang], -1)).astype(np.float32)
    sin[:, :D // 2] = -sin[:, :D // 2]
    by_tile = lambda m: np.ascontiguousarray(m.reshape(NT, P, -1).transpose(1, 0, 2))
    rope0 = np.stack([by_tile(cos), by_tile(sin)], 1).astype(np.float32)
    theta = (np.float32(1.0) / np.float32(10000.0) ** (np.arange(D // 2, dtype=np.float32) / np.float32(D // 2)))
    ang = (np.arange(T, dtype=np.float32)[:, None] * theta[None, :]).astype(np.float32)
    rope1 = np.stack([by_tile(np.cos(ang)), by_tile(np.sin(ang))], 1).astype(np.float32)

    nc = bacc.Bacc("TRN2", target_bir_lowering=False, num_devices=1)
    arrays = {"x_dram": a["x"], "txt_dram": a["txt"], "wpack_dram": wp, "rope0_dram": rope0, "rope1_dram": rope1}
    aps = [nc.dram_tensor(k, v.shape, mb.dt.from_np(v.dtype), kind="ExternalInput").ap() for k, v in arrays.items()]
    wd = nc.dram_tensor("wd_scratch", (B, 9, IMG * IMG), mb.dt.float32, kind="Internal").ap()
    out = nc.dram_tensor("out_dram", (B, T, C), mb.dt.float32, kind="ExternalOutput").ap()
    build(nc, *aps, wd, out)
    r = run(nc, [arrays], core_ids=[0])
    return r.results[0]["out_dram"]
```

```python
import math
from contextlib import ExitStack

import concourse.bass as bass
from concourse import mybir

F32 = mybir.dt.float32
BF16 = mybir.dt.bfloat16
FP16 = mybir.dt.float16
ALU = mybir.AluOpType
ACT = mybir.ActivationFunctionType
AX = mybir.AxisListType.X

P = 128
B = 2
C = 64
IMG = 64
NT = 33
T = NT * P
L = 3
NTRIO = NT // L
W3 = L * P
D = 16
SLOTS = 6
KQ = SLOTS * D
NE, HID = 8, 170
HH = HID // 2
NC3 = 192
LN_EPS = 1e-5
NEG = -1e30
BUFS = 2 * L
LIFT = 14 * math.log(2)

BANK_MAX = 0
BANK_EXP = 3
BANK_OUT = 6
BANK_ROW = 7


class Layer:

    def __init__(self, name, kv, rep, causal, dv, units, qscale):
        self.name, self.kv, self.rep, self.causal, self.dv, self.units = name, kv, rep, causal, dv, units
        self.qscale = qscale
        self.heads = kv * rep
        self.trios = [(j + 1) if causal else NTRIO for j in range(NTRIO)]
        self.steps = L * sum(self.trios)
        self.first = [L * sum(self.trios[:j]) for j in range(NTRIO)]
        self.wide = dv == C
        self.planes = 3 if self.wide else 1
        self.nq = 4 * D if self.wide else self.heads * D
        self.nk = 4 * D if self.wide else kv * D
        self.nv = kv * dv
        self.w = dv + 1
        self.vw = 3 * self.w if self.wide else 4 * self.w


ATT0 = Layer("a0", 4, 1, False, D, B, D ** -0.5)
ATT1 = Layer("a1", 2, 2, True, D, B, D ** -0.5)
ATT2 = Layer("a2", 1, 1, True, C, B, C ** -0.5)
ATT3 = Layer("a3", 1, 4, True, D, B * 4, D ** 0.5)


LAYERS = (ATT0, ATT1, ATT2, ATT3)
for i, later in enumerate(LAYERS):
    later.tiles_before = sum(one.units * one.heads * one.steps for one in LAYERS[:i])
    later.blocks_before = sum(one.units * one.heads * NTRIO for one in LAYERS[:i])


def weight_columns():
    at, out = 0, {}
    for name, n in (("conv1", 16), ("bn", 5), ("conv2", 9), ("wqkv0", 192), ("wo0", 64), ("ln1", 1), ("ln2", 1),
                    ("wqkv1", 128), ("wo1", 64), ("router", NE), ("w1", NE * HID), ("w3", NE * HID),
                    ("w2", 2 * NE * C), ("wcomp", 128), ("wsec", 192), ("hl", 64), ("wn", 4 * 96),
                    ("gate", 16), ("gateb", 16), ("lng", D), ("lnb", D), ("fc1", 64), ("fc2", 64),
                    ("fng", D), ("fnb", D), ("fgate", 4)):
        out[name] = (at, n)
        at += n
    return out, at


COLS, NCOLS = weight_columns()


def build(nc, x, txt, wpack, rope0, rope1, wd_scratch, out):
    outer = ExitStack()
    with outer:
        def sb(name, shape, dt, ctx=outer):
            return ctx.enter_context(nc.sbuf_tensor(name, shape, dt))

        sems = {}

        def sem(name):
            if name not in sems:
                sems[name] = outer.enter_context(nc.semaphore(name))
            return sems[name]

        PS = outer.enter_context(nc.psum_tensor("PS", [P, 8, 512], F32))
        PSH = PS[:, :, :].rearrange("p a b -> p (a b)").bitcast(BF16)

        H = sb("H", [P, B * NT, C], F32)
        WP = sb("WP", [P, NCOLS], F32)
        XN = sb("XN", [P, NT, C], F32)
        XT = sb("XT", [C + 1, W3], F32)
        identf = sb("identf", [P, P], F32)
        identh = sb("identh", [P, P], BF16)
        maskq = sb("maskq", [P, P], BF16)
        maskk = sb("maskk", [P, P], BF16)
        ones2 = sb("ones2", [2, P], BF16)
        st = sb("st", [P, 4, NT], F32)
        bnv = sb("bnv", [16, 4], F32)
        lift = sb("lift", [P, 1], F32)
        MH = sb("MH", [P, NT], F32)

        def wt(name, rows, a=0, n=None):
            at, cols = COLS[name]
            return WP[0:rows, at + a:at + a + (cols - a if n is None else n)]

        tok = ExitStack()
        XC = sb("XC", [C, B, IMG * IMG], F32, tok)
        XS = sb("XS", [P, L, 32, IMG + 2], F32, tok)
        YC = sb("YC", [17, IMG * IMG], F32, tok)
        WD = sb("WD", [9, IMG * IMG], F32, tok)
        WB = sb("WB", [P, 9, IMG], F32, tok)
        TM = sb("TM", [P, 2, 32, IMG], F32, tok)
        tok.close()

        QT = sb("QT", [P, 4, T], BF16)
        KT = sb("KT", [P, 4, T], BF16)
        Yraw = sb("Yraw", [P, NT * 256], F32)
        Y = Yraw[:, :].rearrange("p (t c) -> p t c", c=256)
        Y64 = Yraw[:, 0:NT * C].rearrange("p (t c) -> p t c", c=C)
        VB = Yraw[:, NT * C:NT * 256].bitcast(BF16)
        VB3 = KT[:, 1:4, :].rearrange("p a t -> p (a t)")
        SX = sb("SX", [P, B * NT, C], F32)
        exps_raw = sb("exps_raw", [P, BUFS * W3 * 3 // 2], F32)
        PT = exps_raw[:, 0:BUFS * W3].rearrange("p (l c) -> p l c", l=BUFS)
        PR = exps_raw[:, BUFS * W3:].bitcast(FP16).rearrange("p (l c) -> p l c", l=BUFS)
        PH = exps_raw[:, 0:BUFS * W3].bitcast(BF16).rearrange("p (l c two) -> p l c two", l=BUFS, two=2)[:, :, :, 1]
        OS = sb("OS", [4 * (D + 1), W3], F32)
        SEL = sb("SEL", [4 * (D + 1), D + 1], F32)
        PM = sb("PM", [P, L, NTRIO], F32)
        NM = sb("NM", [P, L], F32)
        MM = sb("MM", [P, L, 2], BF16)
        RC = sb("RC", [P, L], F32)
        STG = sb("STG", [P, L, C], F32)
        YB = sb("YB", [P, L, C], BF16)
        CT = sb("CT", [P, W3], F32)
        QK = sb("QK", [P, L, NC3], F32)
        R1 = sb("R1", [P, L, NC3], F32)
        R2 = sb("R2", [P, L, NC3], F32)
        parts = sb("parts", [P, L * (SLOTS * P + 3 * NC3) // 2], F32)
        halves = parts[:, :].bitcast(BF16)
        C01 = halves[:, 0:3 * L * NC3].rearrange("p (a l c) -> p a l c", a=3, l=L)
        A = halves[:, 3 * L * NC3:3 * L * NC3 + SLOTS * W3].rearrange("p (l c) -> p l c", l=L)
        RT = sb("RT", [P, 2, NT, D], F32)
        G = parts[0:HH, 0:4 * W3].rearrange("p (a b c) -> p a b c", a=2, b=2)
        X1 = sb("X1", [P, L, C], F32)
        OM = sb("OM", [P, L, 256], F32)
        OT = PT[:, 0:2, :]
        E1 = exps_raw[:, BUFS * W3 * 3 // 2 - 8 * L * C:].rearrange("p (a b) -> p a b", a=8)
        S1 = sb("S1", [P, 8, L * 16], F32)
        before = sb("before", [P, NE, NE], F32)[:, :, :]

        bars = [0]

        passed = sem("passed")

        def barrier(eng, k):
            eng.drain()
            eng.sem_inc(sem("met"), 1)
            eng.wait_ge(sem("met"), 4 * k)
            eng.sem_inc(passed, 1)

        MEET_TOK = 2
        BASE0 = MEET_TOK
        BASE1 = BASE0 + 1 + 3 * B
        BASE2 = BASE1 + 1 + 3 * B
        BASE3 = BASE2 + 1 + 3 * B
        MEET3 = 2 * 4 + 1

        def values_of(lay):
            return (VB3 if lay is ATT3 else VB)[:, 0:NT * lay.kv * lay.vw]

        def vtile(lay, kt, kvh, a, n):
            return values_of(lay)[:, bass.ds((kt * lay.kv + kvh) * lay.vw + a, n)]


        def s(lay, what):
            return sem(f"{lay.name}_{what}")

        def plan(lay, j):
            n = lay.trios[j]
            nxt = lay.trios[j + 1] if j + 1 < NTRIO else 0
            lead = nxt - n + 1 if nxt else 0
            if n == 1:
                return [(0, list(range(nxt)))]
            out_ = [(0, list(range(lead + 1)) if nxt else [])]
            out_ += [(t, [t + lead] if nxt else []) for t in range(1, n - 1)]
            return out_ + [(n - 1, [])]

        def share(nexts, r):
            every = [(i, lane) for i in range(len(nexts)) for lane in range(L)]
            return every[r * len(nexts):(r + 1) * len(nexts)]

        def every(eng, lay, j, trio):
            trios = plan(lay, j)
            begin = lay.first[j] // L
            pairs = (len(trios) - (4 if lay.causal else 2)) // 2
            if pairs < 2:
                pairs = 0
            for one in trios[0:2]:
                trio(*one, (begin + one[0]) % 2)
            if pairs:
                shift = trios[1][1][0] - 1 if trios[1][1] else None
                with eng.Fori(0, pairs) as p:
                    for i in (2, 3):
                        t = p * 2 + i
                        trio(t, [t + shift] if shift is not None else [], (begin + i) % 2)
            for one in trios[2 + 2 * pairs:]:
                trio(*one, (begin + one[0]) % 2)

        def outs_beside(lay, j):
            return 1 if lay.trios[j] > 2 and not lay.wide else 0

        def counts(eng, lay, g0, j, t):
            return [eng.snap(g0 + lay.first[j] + t * L + r + 1) for r in range(L)]

        def pe_max(pe, lay, at, h, kvh, j, t, lane):
            diag = lay.causal and isinstance(t, int) and t == lay.trios[j] - 1
            cols = (lane + 1) * P if diag else W3
            pe.wait_ge(sem("maxbank_free"), at[lane])
            for p in range(lay.planes):
                qp, kp = (p, p) if lay.wide else (h, kvh)
                k = P if lay.wide else KQ
                last = not diag and p == lay.planes - 1
                mm = pe.matmul(PS[:, BANK_MAX + lane, 0:cols],
                               QT[0:k].rearrange("p a t -> p (a t)")[:, bass.ds(qp * T + (L * j + lane) * P, P)],
                               KT[0:k].rearrange("p a t -> p (a t)")[:, bass.ds(kp * T + t * W3, cols)],
                               start=p == 0, stop=last, skip_group_check=True)
            if diag:
                mm = pe.matmul(PS[:, BANK_MAX + lane, lane * P:cols], identh[:, :], maskq[:, :],
                               start=False, stop=True, skip_group_check=True)
            mm.then_inc(sem("maxscores"), 1)

        def pe_score(pe, lay, at, h, kvh, j, t, r):
            diag = lay.causal and isinstance(t, int) and t == lay.trios[j] - 1
            c0 = r * P if diag else 0
            pe.wait_ge(sem("exps"), at[r])
            for p in range(lay.planes):
                qp, kp = (p, p) if lay.wide else (h, kvh)
                k = P if lay.wide else KQ + 2
                last = not diag and not lay.wide
                mm = pe.matmul(PS[:, BANK_EXP + r, c0:W3],
                               KT[0:k].rearrange("p a t -> p (a t)")[:, bass.ds(kp * T + (t * L + r) * P, P)],
                               QT[0:k].rearrange("p a t -> p (a t)")[:, bass.ds(qp * T + j * W3 + c0, W3 - c0)],
                               start=p == 0, stop=last, skip_group_check=True)
            if lay.wide:
                mm = pe.matmul(PS[:, BANK_EXP + r, c0:W3], ones2[:, :],
                               QT[0:2, 3, j * W3 + c0:(j + 1) * W3],
                               start=False, stop=not diag, skip_group_check=True)
            if diag:
                mm = pe.matmul(PS[:, BANK_EXP + r, c0:c0 + P], identh[:, :], maskk[:, :],
                               start=False, stop=True, skip_group_check=True)
            mm.then_inc(sem("scores"), 1)

        def pe_values(pe, lay, at, b0, kvh, j, t, half, r):
            first = r == 0 and isinstance(t, int) and t == 0
            last = r == 2 and isinstance(t, int) and t == lay.trios[j] - 1
            buf = half * L + r
            diag = lay.causal and isinstance(t, int) and t == lay.trios[j] - 1
            l0 = r if diag else 0
            if r == 0:
                pe.wait_ge(sem("rests_dve"), at[0])
            else:
                pe.wait_ge(sem("rests_pool"), at[r])
            if first:
                pe.wait_ge(sem("out_free"), b0 + j + 1)
            if lay.wide:
                for lane in range(l0, L):
                    for source in (PH, PR):
                        for part in range(3):
                            mm = pe.matmul(PS[:, BANK_OUT, lane * lay.w:(lane + 1) * lay.w],
                                           source[:, buf, lane * P:(lane + 1) * P],
                                           vtile(lay, t * L + r, kvh, part * lay.w, lay.w),
                                           start=first and lane == 0 and source is PH and part == 0,
                                           stop=last and source is PR and part == 2, skip_group_check=True)
            else:
                for source in (PH, PR):
                    mm = pe.matmul(PS[0:lay.vw, BANK_OUT, l0 * P:W3], vtile(lay, t * L + r, kvh, 0, lay.vw),
                                   source[:, buf, l0 * P:W3], start=first and source is PH,
                                   stop=last and source is PR, skip_group_check=True)
            mm.then_inc(sem("values"), 1)

        def pe_outs(pe, lay, b0, j):
            pe.wait_ge(sem("out_free"), b0 + j + 2)
            pe.wait_ge(s(lay, "outs_put"), b0 + j + 1 - lay.blocks_before)
            for lane in range(L):
                mm = pe.matmul(PS[:, BANK_ROW, lane * lay.w:(lane + 1) * lay.w], OS[:, lane * P:(lane + 1) * P],
                               SEL[:, :], start=True, stop=True)
            mm.then_inc(s(lay, "outs"), 1)

        def pe_maxrow(pe, lay, b0, j):
            pe.wait_ge(sem("negmax"), b0 + j + 1)
            for lane in range(L):
                mm = pe.matmul(PS[0:2, BANK_ROW, lane * P:(lane + 1) * P], MM[:, lane, :], identh[:, :],
                               start=True, stop=True)
            mm.then_inc(sem("maxrow"), 1)

        def pe_head(pe, lay, u, kvh, rr):
            h = kvh * lay.rep + rr
            g0 = (u * lay.heads + h) * lay.steps + lay.tiles_before
            b0 = (u * lay.heads + h) * NTRIO + lay.blocks_before
            if lay.causal:
                at = counts(pe, lay, g0, 0, 0)
                for lane in range(L):
                    pe_max(pe, lay, at, h, kvh, 0, 0, lane)
            else:
                with pe.Fori(0, NTRIO) as t:
                    at = counts(pe, lay, g0, 0, t)
                    for lane in range(L):
                        pe_max(pe, lay, at, h, kvh, 0, t, lane)
            pe_maxrow(pe, lay, b0, 0)
            every_h, every_kvh = h, kvh
            own = [pe.alloc_register(f"{lay.name}_{i}") for i in range(2)]
            for j in range(NTRIO):
                if not isinstance(every_h, int):
                    pe.reg_mov(own[0], every_h)
                    h = pe.snap(own[0], min_val=0, max_val=lay.heads - 1)
                if not isinstance(every_kvh, int):
                    pe.reg_mov(own[1], every_kvh)
                    kvh = pe.snap(own[1], min_val=0, max_val=lay.kv - 1)

                def trio(t, nexts, half):
                    at = counts(pe, lay, g0, j, t)
                    to = [counts(pe, lay, g0, j + 1, t2) for t2 in nexts]
                    for r in range(L):
                        for i, lane in share(nexts, r):
                            pe_max(pe, lay, to[i], h, kvh, j + 1, nexts[i], lane)
                        if r == 2 and j > 0 and isinstance(t, int) and t == 1 == outs_beside(lay, j):
                            pe_outs(pe, lay, b0, j - 1)
                        if r == 2 and j + 1 < NTRIO and isinstance(t, int) and t == lay.trios[j] - 1:
                            pe_maxrow(pe, lay, b0, j + 1)
                        first = isinstance(t, int) and t == 0
                        if first and r == 0:
                            pe.wait_ge(sem("maxrow_set"), b0 + j + 1)
                            pe.sem_inc(passed, 1)
                        pe_score(pe, lay, at, h, kvh, j, t, r)
                        if not first:
                            pe_values(pe, lay, at, b0, kvh, j, t - 1, 1 - half, r)
                        elif j > 0:
                            pe_values(pe, lay, at, b0, kvh, j - 1, lay.trios[j - 1] - 1, 1 - half, r)
                    if first and j > 0 and not lay.wide and outs_beside(lay, j) == 0:
                        pe_outs(pe, lay, b0, j - 1)

                every(pe, lay, j, trio)
            at = counts(pe, lay, g0, NTRIO - 1, lay.trios[-1])
            for r in range(L):
                pe_values(pe, lay, at, b0, kvh, NTRIO - 1, lay.trios[-1] - 1, (lay.steps // L - 1) % 2, r)
            if not lay.wide:
                pe_outs(pe, lay, b0, NTRIO - 1)

        def act_head(act, lay, u, kvh, rr):
            g0 = (u * lay.heads + kvh * lay.rep + rr) * lay.steps + lay.tiles_before

            def exps(at, half, r, diag):
                c0 = r * P if diag else 0
                act.wait_ge(sem("scores"), at[r])
                act.wait_ge(sem("values"), at[r])
                act.activation(PT[:, half * L + r, c0:W3], PS[:, BANK_EXP + r, c0:W3], ACT.Exp, bias=lift[:, 0:1])\
                   .then_inc(sem("exps"), 1)

            def take_outs(j):
                act.wait_ge(sem("values"), g0 + lay.first[j] + L * lay.trios[j] + BUFS)
                act.activation(OS[:, :], PS[0:lay.vw, BANK_OUT, 0:W3], ACT.Copy).then_inc(sem("out_free"), 1)

            act.wait_ge(sem("values"), g0 + BUFS)
            act.sem_inc(passed, 1)
            for j in range(NTRIO):

                def trio(t, nexts, half):
                    at = counts(act, lay, g0, j, t)
                    for r in range(L):
                        exps(at, half, r, lay.causal and isinstance(t, int) and t == lay.trios[j] - 1)
                    if isinstance(t, int) and t == 0 and j > 0 and not lay.wide:
                        take_outs(j - 1)

                every(act, lay, j, trio)
            if not lay.wide:
                take_outs(NTRIO - 1)

        def pool_head(pool, lay, u, kvh, rr):
            g0 = (u * lay.heads + kvh * lay.rep + rr) * lay.steps + lay.tiles_before

            for j in range(NTRIO):

                def trio(t, nexts, half):
                    at = counts(pool, lay, g0 + L, j, t)
                    for r in (1, 2):
                        c0 = r * P if lay.causal and isinstance(t, int) and t == lay.trios[j] - 1 else 0
                        buf = half * L + r
                        pool.wait_ge(sem("exps"), at[r])
                        pool.tensor_tensor(PR[:, buf, c0:W3], PT[:, buf, c0:W3], PH[:, buf, c0:W3], ALU.subtract)\
                            .then_inc(sem("rests_pool"), r)

                every(pool, lay, j, trio)

        def dve_max(dve, lay, at, j, t, lane):
            diag = lay.causal and isinstance(t, int) and t == lay.trios[j] - 1
            cols = (lane + 1) * P if diag else W3
            dve.wait_ge(sem("maxscores"), at[lane])
            dve.tensor_reduce(PM[:, lane, bass.ds(t, 1)], PS[:, BANK_MAX + lane, 0:cols], AX, ALU.max)\
               .then_inc(sem("maxbank_free"), 1)

        def dve_rest(dve, lay, g0, j, t, half):
            dve.wait_ge(sem("exps"), g0 + lay.first[j] + t * L + 1 + L)
            buf = half * L
            dve.tensor_tensor(PR[:, buf, :], PT[:, buf, :], PH[:, buf, :], ALU.subtract).then_inc(sem("rests_dve"), L)

        def dve_negmax(dve, lay, j):
            dve.drain()
            dve.tensor_reduce(NM[:, :], PM[:, :, 0:lay.trios[j]], AX, ALU.max, negate=True)
            dve.drain()
            dve.tensor_copy(MM[:, :, 0], NM[:, :])
            dve.drain()
            dve.tensor_tensor(MM[:, :, 1], NM[:, :], MM[:, :, 0], ALU.subtract).then_inc(sem("negmax"), 1)

        def dve_rows(dve, lay, b0, h, j):
            dve.wait_ge(sem("maxrow"), b0 + j + 1)
            if lay.wide:
                dst = QT[0:2, 3, j * W3:(j + 1) * W3]
            else:
                dst = QT[KQ:KQ + 2].rearrange("p a t -> p (a t)")[:, bass.ds(h * T + j * W3, W3)]
            dve.tensor_copy(dst, PS[0:2, BANK_ROW, 0:W3]).then_inc(sem("maxrow_set"), 1)

        def dve_out(dve, lay, g0, b0, h, j):
            if lay.wide:
                dve.wait_ge(sem("values"), g0 + lay.first[j] + L * lay.trios[j] + BUFS)
                bank = BANK_OUT
            else:
                dve.wait_ge(s(lay, "outs"), b0 + j + 1 - lay.blocks_before)
                bank = BANK_ROW
            acc = PS[:, bank, 0:L * lay.w].rearrange("p (l w) -> p l w", w=lay.w)
            y = Y if lay is ATT3 else Y64
            dve.reciprocal(RC[:, :], acc[:, :, lay.dv])
            dve.drain()
            dve.tensor_tensor(y[:, L * j:L * j + L, bass.ds(h * lay.dv, lay.dv)], acc[:, :, 0:lay.dv],
                              RC[:, :].unsqueeze(2).broadcast_to([P, L, lay.dv]), ALU.mult)\
               .then_inc(sem("out_free") if lay.wide else s(lay, "outs_put"), 1)

        def dve_head(dve, lay, u, kvh, rr, yh):
            h = kvh * lay.rep + rr
            g0 = (u * lay.heads + h) * lay.steps + lay.tiles_before
            b0 = (u * lay.heads + h) * NTRIO + lay.blocks_before
            if lay.causal:
                at = counts(dve, lay, g0, 0, 0)
                for lane in range(L):
                    dve_max(dve, lay, at, 0, 0, lane)
            else:
                with dve.Fori(0, NTRIO) as t:
                    at = counts(dve, lay, g0, 0, t)
                    for lane in range(L):
                        dve_max(dve, lay, at, 0, t, lane)
            dve_negmax(dve, lay, 0)
            dve_rows(dve, lay, b0, h, 0)
            for j in range(NTRIO):

                def trio(t, nexts, half):
                    to = [counts(dve, lay, g0, j + 1, t2) for t2 in nexts]
                    last = j + 1 < NTRIO and isinstance(t, int) and t == lay.trios[j] - 1
                    if last and t > 0:
                        dve_negmax(dve, lay, j + 1)
                    for r in range(L):
                        if r == 1:
                            dve_rest(dve, lay, g0, j, t, half)
                        for i, lane in share(nexts, r):
                            dve_max(dve, lay, to[i], j + 1, nexts[i], lane)
                    if last and t == 0:
                        dve_negmax(dve, lay, j + 1)
                    if isinstance(t, int) and t == outs_beside(lay, j) and j > 0:
                        dve_out(dve, lay, g0, b0, yh, j - 1)

                every(dve, lay, j, trio)
                if j + 1 < NTRIO:
                    dve_rows(dve, lay, b0, h, j + 1)
            dve_out(dve, lay, g0, b0, yh, NTRIO - 1)

        def heads(eng, lay, body):
            if lay.kv > 1 and lay.rep > 1:
                with eng.Fori(0, lay.kv) as kvh:
                    with eng.Fori(0, lay.rep) as rr:
                        body(kvh, rr)
            elif lay.kv > 1:
                with eng.Fori(0, lay.kv) as kvh:
                    body(kvh, 0)
            elif lay.rep > 1:
                with eng.Fori(0, lay.rep) as rr:
                    body(0, rr)
            else:
                body(0, 0)


        def ask_rstd(dve, what, k):
            dve.drain()
            dve.sem_inc(sem(what + "_var"), 1)
            dve.wait_ge(sem(what + "_rstd"), k + 1)
            dve.sem_inc(passed, 1)

        def pool_rstd(pool, what, k, n, eps):
            pool.wait_ge(sem(what + "_var"), k + 1)
            pool.sem_inc(passed, 1)
            pool.tensor_scalar(st[:, 1, 0:n], st[:, 3, 0:n], eps, None, ALU.add)
            pool.drain()
            pool.tensor_tensor(st[:, 2, 0:n], st[:, 1, 0:n], MH[:, 0:n], ALU.pow)\
                .then_inc(sem(what + "_rstd"), 1)

        def dve_layernorm(dve, b, what, sq):
            hb = H[:, bass.ds(b * NT, NT), :]
            dve.tensor_reduce(st[:, 0, :], hb, AX, ALU.add)
            dve.drain()
            dve.tensor_scalar(st[:, 1, :], st[:, 0, :], 1.0 / C, None, ALU.mult)
            dve.drain()
            dve.tensor_tensor(XN[:, :, :], hb, st[:, 1, :].unsqueeze(2).broadcast_to([P, NT, C]), ALU.subtract)
            dve.drain()
            dve.tensor_tensor(sq, XN[:, :, :], XN[:, :, :], ALU.mult)
            dve.drain()
            dve.tensor_reduce(st[:, 2, :], sq, AX, ALU.add)
            dve.drain()
            dve.tensor_scalar(st[:, 3, :], st[:, 2, :], 1.0 / C, None, ALU.mult)
            ask_rstd(dve, what, b)
            dve.tensor_tensor(XN[:, :, :], XN[:, :, :], st[:, 2, :].unsqueeze(2).broadcast_to([P, NT, C]), ALU.mult)
            dve.drain()

        def dve_split(dve, lay, it):
            n = lay.nq + lay.nk + lay.nv
            q, r1 = QK[:, :, 0:n], R1[:, :, 0:n]
            dve.tensor_copy(C01[:, 0, :, 0:n], q)
            dve.drain()
            dve.tensor_tensor(r1, q, C01[:, 0, :, 0:n], ALU.subtract)
            dve.drain()
            dve.tensor_copy(C01[:, 1, :, 0:n], r1)
            dve.drain()
            dve.tensor_tensor(C01[:, 2, :, 0:n], r1, C01[:, 1, :, 0:n], ALU.subtract).then_inc(s(lay, "parts"), 1)
            dve.drain()
            copies = slots(lay, 0)
            for dst, part in copies[:-1]:
                dve.tensor_copy(dst, part)
            dve.tensor_copy(*copies[-1]).then_inc(s(lay, "query_slots"), 1)

        def slots(lay, which):
            c0, n = ((0, lay.nq), (lay.nq, lay.nk))[which]
            d = C if lay.wide else D
            to = A[:, :, c0 * SLOTS:(c0 + n) * SLOTS].rearrange("p l (h s d) -> p l h s d", s=SLOTS, d=d)
            order = ((0, 0, 1, 1, 0, 2), (0, 1, 0, 1, 2, 0))[which]
            return [(to[:, :, :, slot, :], C01[:, part, :, c0:c0 + n].rearrange("p l (h d) -> p l h d", d=d))
                    for slot, part in enumerate(order)]

        def pool_slots(pool, lay, it):
            pool.wait_ge(s(lay, "parts"), it + 1)
            pool.sem_inc(passed, 1)
            for dst, part in slots(lay, 1):
                pool.tensor_copy(dst, part)
            pool.drain()
            pool.sem_inc(s(lay, "key_slots"), 1)

        def act_values(act, lay, it, t):
            act.wait_ge(s(lay, "parts"), it + 1)
            act.sem_inc(passed, 1)
            at = lay.nq + lay.nk
            v = values_of(lay).rearrange("p (t k w) -> p t k w", k=lay.kv, w=lay.vw)
            for part in range(3):
                last = act.activation(v[:, bass.ds(t * L, L), :, part * lay.w:part * lay.w + lay.dv],
                                      C01[:, part, :, at:at + lay.nv].rearrange("p l (k d) -> p l k d", d=lay.dv),
                                      ACT.Copy)
            last.then_inc(s(lay, "value_parts"), 1)

        def pe_turn(pe, lay, it):
            pe.wait_ge(s(lay, "query_slots"), it + 1)
            pe.wait_ge(s(lay, "key_slots"), it + 1)
            pe.wait_ge(s(lay, "value_parts"), it + 1)
            pe.sem_inc(passed, 1)
            for base, c0, n in ((4 * 1024, 0, lay.nq), (6 * 1024, lay.nq, lay.nk)):
                if lay.wide:
                    for p in range(3):
                        for l in range(L):
                            mm = pe.transpose(PSH[:, base + (p * L + l) * P:base + (p * L + l + 1) * P],
                                              A[:, l, c0 * SLOTS + p * P:c0 * SLOTS + (p + 1) * P], identh[:, :])
                else:
                    for i in range(n // D):
                        for l in range(L):
                            mm = pe.transpose(PSH[0:KQ, base + (i * L + l) * P:base + (i * L + l + 1) * P],
                                              A[:, l, c0 * SLOTS + i * KQ:c0 * SLOTS + (i + 1) * KQ], identh[:, :])
            mm.then_inc(s(lay, "turned"), 1)

        def put_turned(eng, lay, it, t, which):
            if which == 0:
                act_values(eng, lay, it, t)
            eng.wait_ge(s(lay, "turned"), it + 1)
            eng.sem_inc(passed, 1)
            rows = P if lay.wide else KQ
            n = 3 if lay.wide else (lay.nq if which == 0 else lay.nk) // D
            dst, base = (QT, 4 * 1024) if which == 0 else (KT, 6 * 1024)
            o = dst[0:rows, 0:n, bass.ds(t * W3, W3)]
            i = PSH[0:rows, base:base + n * W3].rearrange("p (a t) -> p a t", t=W3)
            if which == 0:
                eng.activation(o, i, ACT.Copy).then_inc(s(lay, "put"), 1)
            else:
                eng.tensor_copy(o, i).then_inc(s(lay, "put"), 1)

        block = outer.enter_context(nc.Block())

        @block.sync
        def _(sp):
            sp.dma_start(WP[:, :], wpack).then_inc(sem("weights_in"), 16)
            for b in range(B):
                sp.dma_start(XC[:, b, :], x[b].rearrange("c h w -> c (h w)")).then_inc(sem("image_in"), 16)
            for b in range(B):
                sp.dma_start(H[:, b * NT + NT - 1, :], txt[b]).then_inc(sem("text_in"), 16)
            xr = x.rearrange("b (t c) h w -> b c h t w", c=2)
            for b in range(B):
                sp.wait_ge(sem("shift_free"), b + 1)
                for i in range(3):
                    lo, hi = max(0, 1 - i), min(IMG, IMG + 1 - i)
                    for c2 in range(2):
                        for hf in range(2):
                            a_, z_ = (lo, 32) if hf == 0 else (32, hi)
                            for t0 in range(0, 32, 16):
                                sp.dma_start(XS[c2 * IMG + a_:c2 * IMG + z_, i, t0:t0 + 16, 1:IMG + 1],
                                             xr[b, c2, a_ + i - 1:z_ + i - 1, t0:t0 + 16, :])\
                                  .then_inc(sem("shift_in"), 16)
                sp.wait_ge(sem("dyn"), b + 1)
                sp.dma_start(wd_scratch[b], WD[:, :]).then_inc(sem("dyn_out"), 16)
                sp.wait_ge(sem("dyn_out"), 16 * (b + 1))
                for c2 in range(2):
                    sp.dma_start(WB[c2 * IMG:(c2 + 1) * IMG, :, :],
                                 wd_scratch[b].rearrange("k (h w) -> h k w", w=IMG)).then_inc(sem("rows_in"), 16)
            sp.wait_ge(sem("table_free"), 1)
            sp.dma_start(RT[:, :, :, :], rope0).then_inc(sem("table_in"), 16)
            sp.wait_ge(sem("table_free"), 2)
            sp.dma_start(RT[:, :, :, 0:D // 2], rope1).then_inc(sem("table_in"), 16)
            sp.wait_ge(sem("final"), 1)
            for b in range(B):
                sp.dma_start(out[b].rearrange("(t p) w -> p t w", p=P), H[:, b * NT:(b + 1) * NT, :])\
                  .then_inc(sem("stored"), 16)
            sp.wait_ge(sem("stored"), 16 * B)
            sp.wait_ge(sem("table_in"), 16 * 2)

        @block.gpsimd
        def _(pool):
            pool.wait_ge(sem("weights_in"), 16)
            pool.sem_inc(passed, 1)
            pool.memset(MH[:, :], -0.5)
            pool.memset(lift[:, :], LIFT)
            pool.tensor_scalar(bnv[:, 0:1], wt("bn", 16, 3, 1), 1e-5, None, ALU.add)
            pool.drain()
            pool.tensor_tensor(bnv[:, 2:3], bnv[:, 0:1], MH[0:16, 0:1], ALU.pow).then_inc(sem("bn_rstd"), 1)
            pool.memset(XS[:, :, :, :].rearrange("p a b c -> p (a b c)"), 0.0).then_inc(sem("shift_free"), 1)
            pool.memset(YC[:, :], 1.0).then_inc(sem("ones_row"), 1)
            pool.memset(identf[:, :], 0.0)
            pool.memset(SEL[:, :], 0.0)
            pool.drain()
            pool.memset(maskq[:, :], 0.0)
            pool.memset(maskk[:, :], 0.0)
            pool.drain()
            pool.memset(ones2[:, :], 1.0)
            pool.drain()
            pool.memset(XT[C:C + 1, :], 1.0)
            pool.drain()
            pool.affine_select(out=identf[:, :], in_=identf[:, :], compare_op=ALU.not_equal, fill=1.0, base=0,
                               pattern=[[-1, P]], channel_multiplier=1)
            for part in range(3):
                pool.affine_select(out=SEL[:, :], in_=SEL[:, :], compare_op=ALU.not_equal, fill=1.0,
                                   base=-part * (D + 1), pattern=[[-1, D + 1]], channel_multiplier=1)
                pool.drain()
            pool.affine_select(out=maskq[:, :], in_=maskq[:, :], compare_op=ALU.is_ge, fill=NEG, base=0,
                               pattern=[[-1, P]], channel_multiplier=1)
            pool.affine_select(out=maskk[:, :], in_=maskk[:, :], compare_op=ALU.is_ge, fill=NEG, base=0,
                               pattern=[[1, P]], channel_multiplier=-1)
            pool.drain()
            pool.tensor_copy(identh[:, :], identf[:, :])
            barrier(pool, 1)
            barrier(pool, 2)
            pool.sem_inc(sem("table_free"), 1)

            def ones(lay, k):
                pool.memset(values_of(lay), 0.0)
                pool.drain()
                pool.memset(values_of(lay).rearrange("p (n w) -> p n w", w=lay.vw)[:, :, lay.dv:lay.dv + 1], 1.0)
                pool.drain()
                if not lay.wide:
                    pool.memset(KT[KQ:KQ + 2, 0:lay.kv, :], 1.0)
                barrier(pool, k)

            ones(ATT0, BASE0 + 1)
            with pool.Fori(0, B) as b:
                pool_rstd(pool, "ln0", b, NT, LN_EPS)
                with pool.Fori(0, NTRIO) as t:
                    pool_slots(pool, ATT0, b * NTRIO + t)
                barrier(pool, BASE0 + 2 + 3 * b)
                heads(pool, ATT0, lambda kvh, rr: pool_head(pool, ATT0, b, kvh, rr))
                barrier(pool, BASE0 + 3 + 3 * b)
                with pool.Fori(0, NTRIO) as t:
                    pool.wait_ge(sem("p0_done"), b * NTRIO + t + 1)
                    pool.sem_inc(passed, 1)
                    pool.tensor_copy(YB[:, :, :], Y64[:, bass.ds(t * L, L), :]).then_inc(sem("p0_y"), 1)
                barrier(pool, BASE0 + 4 + 3 * b)

            ones(ATT1, BASE1 + 1)
            with pool.Fori(0, B) as b:
                pool_rstd(pool, "ln1", b, NT, LN_EPS)
                pool_rstd(pool, "rms", b, NT, 1e-6)
                with pool.Fori(0, NTRIO) as t:
                    pool_slots(pool, ATT1, b * NTRIO + t)
                barrier(pool, BASE1 + 2 + 3 * b)
                heads(pool, ATT1, lambda kvh, rr: pool_head(pool, ATT1, b, kvh, rr))
                barrier(pool, BASE1 + 3 + 3 * b)
                with pool.Fori(0, NTRIO) as t:
                    pool_rstd(pool, "rm1", b * NTRIO + t, L, 1e-6)
                barrier(pool, BASE1 + 4 + 3 * b)
            pool.sem_inc(sem("table_free"), 1)
            ones(ATT2, BASE2 + 1)
            with pool.Fori(0, B) as b:
                pool_rstd(pool, "ln2", b, NT, LN_EPS)
                with pool.Fori(0, NTRIO) as t:
                    pool_slots(pool, ATT2, b * NTRIO + t)
                barrier(pool, BASE2 + 2 + 3 * b)
                heads(pool, ATT2, lambda kvh, rr: pool_head(pool, ATT2, b, kvh, rr))
                barrier(pool, BASE2 + 3 + 3 * b)
                barrier(pool, BASE2 + 4 + 3 * b)
            ones(ATT3, BASE3 + 1)
            with pool.Fori(0, B) as b:
                pool_rstd(pool, "ln3", b, NT, LN_EPS)
            barrier(pool, BASE3 + 2)
            with pool.Fori(0, B) as b:
                with pool.Fori(0, 4) as n:
                    with pool.Fori(0, NTRIO) as t:
                        it = (b * 4 + n) * NTRIO + t
                        pool.wait_ge(sem("a3_stage_free"), it + 1)
                        pool.sem_inc(passed, 1)
                        pool.tensor_copy(STG[:, :, 0:D], SX[:, bass.ds(b * NT + t * L, L), bass.ds(n * D, D)])\
                            .then_inc(s(ATT3, "stage"), 1)
                        pool_slots(pool, ATT3, it)
                    barrier(pool, BASE3 + 3 + MEET3 * b + 2 * n)
                    heads(pool, ATT3, lambda kvh, rr: pool_head(pool, ATT3, b * 4 + n, kvh, rr))
                    barrier(pool, BASE3 + 4 + MEET3 * b + 2 * n)
                with pool.Fori(0, NTRIO) as t:
                    for i in range(2):
                        pool_rstd(pool, "n16", (b * NTRIO + t) * 2 + i, L * 4, 1e-8)
                barrier(pool, BASE3 + 3 + MEET3 * b + 8)

        @block.tensor
        def _(pe):
            pe.wait_ge(sem("weights_in"), 16)
            pe.sem_inc(passed, 1)
            for b in range(B):
                pe.wait_ge(sem("image_in"), 16 * B)
                pe.sem_inc(passed, 1)
                if b:
                    pe.wait_ge(sem("dyn"), b)
                    pe.sem_inc(passed, 1)
                for k in range(8):
                    mm = pe.matmul(PS[0:16, k, :], wt("conv1", C), XC[:, b, k * 512:(k + 1) * 512], start=True, stop=True)
                mm.then_inc(sem("conv1"), 1)
                pe.wait_ge(sem("relu"), b + 1)
                pe.sem_inc(passed, 1)
                for k in range(8):
                    mm = pe.matmul(PS[0:9, k, :], wt("conv2", 17), YC[:, k * 512:(k + 1) * 512], start=True, stop=True)
                mm.then_inc(sem("conv2"), 1)
            barrier(pe, 1)
            barrier(pe, 2)

            def transpose3(src, what, it, ident=identf, width=C):
                pe.wait_ge(sem(what + "_in"), it + 1)
                pe.sem_inc(passed, 1)
                for l in range(L):
                    o = PS[0:width, 0, l * P:(l + 1) * P] if ident is identf else PSH[0:width, l * P:(l + 1) * P]
                    mm = pe.transpose(o, src[:, l, 0:width], ident[:, :])
                mm.then_inc(sem(what + "_t"), 1)

            def project3(what, it, k, w, n, src=None):
                pe.wait_ge(sem(what + "_ts"), it + 1)
                pe.sem_inc(passed, 1)
                x_ = XT if src is None else src
                for l in range(L):
                    mm = pe.matmul(PS[:, 1 + l, 0:n], x_[0:k, l * P:(l + 1) * P], w, start=True, stop=True)
                mm.then_inc(sem(what + "_p"), 1)

            barrier(pe, BASE0 + 1)
            with pe.Fori(0, B) as b:
                with pe.Fori(0, NTRIO) as t:
                    it = b * NTRIO + t
                    transpose3(STG, "a0", it)
                    project3("a0", it, C + 1, wt("wqkv0", C + 1), 192)
                    pe_turn(pe, ATT0, it)
                barrier(pe, BASE0 + 2 + 3 * b)
                heads(pe, ATT0, lambda kvh, rr: pe_head(pe, ATT0, b, kvh, rr))
                barrier(pe, BASE0 + 3 + 3 * b)
                with pe.Fori(0, NTRIO) as t:
                    it = b * NTRIO + t
                    pe.wait_ge(sem("p0_y"), it + 1)
                    pe.sem_inc(passed, 1)
                    for l in range(L):
                        mm = pe.transpose(PSH[0:C, l * P:(l + 1) * P], YB[:, l, :], identh[:, :])
                    mm.then_inc(sem("p0_t"), 1)
                    project3("p0", it, C + 1, wt("wo0", C + 1), C)
                barrier(pe, BASE0 + 4 + 3 * b)

            barrier(pe, BASE1 + 1)
            with pe.Fori(0, B) as b:
                with pe.Fori(0, NTRIO) as t:
                    it = b * NTRIO + t
                    transpose3(STG, "a1", it)
                    project3("a1", it, C, wt("wqkv1", C), 128)
                    pe_turn(pe, ATT1, it)
                barrier(pe, BASE1 + 2 + 3 * b)
                heads(pe, ATT1, lambda kvh, rr: pe_head(pe, ATT1, b, kvh, rr))
                barrier(pe, BASE1 + 3 + 3 * b)
                with pe.Fori(0, NTRIO) as t:
                    it = b * NTRIO + t
                    transpose3(STG, "p1", it)
                    project3("p1", it, C, wt("wo1", C), C)
                    transpose3(OM, "m", it)
                    project3("m", it, C, wt("router", C), NE)
                    pe.wait_ge(sem("m_router_read"), it + 1)
                    pe.sem_inc(passed, 1)
                    for e in range(NE + 1):
                        if e < NE:
                            for hf in range(2):
                                i = 2 * e + hf
                                pe.wait_ge(sem("m_g"), it * 16 + i + 1)
                                pe.sem_inc(passed, 1)
                                for k, name in enumerate(("w1", "w3")):
                                    mm = pe.matmul(PS[0:HH, 2 * (i % 3) + k, 0:W3],
                                                   wt(name, C, e * HID + hf * HH, HH), XT[0:C, :],
                                                   start=True, stop=True)
                                mm.then_inc(sem("m_ab"), 1)
                        if e > 0:
                            f = e - 1
                            pe.wait_ge(sem("m_g"), it * 16 + 2 * f + 2 + 3)
                            pe.sem_inc(passed, 1)
                            pe.wait_ge(sem("m_acc"), it * NE + f + 1)
                            pe.sem_inc(passed, 1)
                            for l in range(L):
                                for hf in range(2):
                                    mm = pe.matmul(PS[:, 6 + f % 2, l * C:(l + 1) * C],
                                                   G[:, f % 2, hf, l * P:(l + 1) * P],
                                                   wt("w2", HH, (hf * NE + f) * C, C), start=hf == 0, stop=hf == 1)
                            mm.then_inc(sem("m_o"), 1)
                barrier(pe, BASE1 + 4 + 3 * b)
            barrier(pe, BASE2 + 1)
            with pe.Fori(0, B) as b:
                with pe.Fori(0, NTRIO) as t:
                    it = b * NTRIO + t
                    transpose3(STG, "a2", it)
                    pe.wait_ge(sem("a2_ts"), it + 1)
                    pe.sem_inc(passed, 1)
                    pe.matmul(PS[:, 1, 0:W3], wt("wcomp", C), XT[0:C, :], start=True, stop=True)\
                      .then_inc(sem("a2_c"), 1)
                    project3("a2c", it, P, wt("wsec", P), 192, CT)
                    pe_turn(pe, ATT2, it)
                barrier(pe, BASE2 + 2 + 3 * b)
                heads(pe, ATT2, lambda kvh, rr: pe_head(pe, ATT2, b, kvh, rr))
                barrier(pe, BASE2 + 3 + 3 * b)
                barrier(pe, BASE2 + 4 + 3 * b)
            barrier(pe, BASE3 + 1)
            with pe.Fori(0, B) as b:
                with pe.Fori(0, NTRIO) as t:
                    it = b * NTRIO + t
                    transpose3(STG, "sx", it)
                    project3("sx", it, C + 1, wt("hl", C + 1), C)
            barrier(pe, BASE3 + 2)
            with pe.Fori(0, B) as b:
                with pe.Fori(0, 4) as n:
                    with pe.Fori(0, NTRIO) as t:
                        it = (b * 4 + n) * NTRIO + t
                        pe.wait_ge(s(ATT3, "stage"), it + 1)
                        pe.sem_inc(passed, 1)
                        for l in range(L):
                            mm = pe.transpose(PS[0:D, 0, l * P:(l + 1) * P], STG[:, l, 0:D], identf[:, :])
                        mm.then_inc(sem("a3_t"), 1)
                        pe.wait_ge(sem("a3_ts"), it + 1)
                        pe.sem_inc(passed, 1)
                        at = COLS["wn"][0]
                        for l in range(L):
                            mm = pe.matmul(PS[:, 1 + l, 0:96], XT[0:D, l * P:(l + 1) * P],
                                           WP[0:D, bass.ds(n * 96 + at, 96)], start=True, stop=True)
                        mm.then_inc(sem("a3_p"), 1)
                        pe_turn(pe, ATT3, it)
                    barrier(pe, BASE3 + 3 + MEET3 * b + 2 * n)
                    heads(pe, ATT3, lambda kvh, rr: pe_head(pe, ATT3, b * 4 + n, kvh, rr))
                    barrier(pe, BASE3 + 4 + MEET3 * b + 2 * n)
                with pe.Fori(0, NTRIO) as t:
                    it = b * NTRIO + t
                    pe.wait_ge(sem("p3_om"), it + 1)
                    pe.sem_inc(passed, 1)
                    for hp in range(2):
                        for l in range(L):
                            mm = pe.transpose(PS[:, hp, l * P:(l + 1) * P], OM[:, l, hp * P:(hp + 1) * P], identf[:, :])
                    mm.then_inc(sem("p3_omt"), 1)
                    pe.wait_ge(sem("p3_ot"), it + 1)
                    pe.sem_inc(passed, 1)
                    for l in range(L):
                        for hp in range(2):
                            mm = pe.matmul(PS[:, 2, (2 * l + hp) * 8:(2 * l + hp + 1) * 8], OT[:, hp, l * P:(l + 1) * P],
                                           wt("gate", P, hp * 8, 8), start=True, stop=True)
                    mm.then_inc(sem("p3_gate"), 1)
                    for i, (w, k, n_) in enumerate((("fc1", C + 1, C), ("fc2", C + 1, C), ("fgate", C, 4))):
                        transpose3(STG, "p3", it * 3 + i)
                        project3("p3", it * 3 + i, k, wt(w, k), n_)
                barrier(pe, BASE3 + 3 + MEET3 * b + 8)

        @block.scalar
        def _(act):
            act.preload_act_table(ACT.Exp)
            act.wait_ge(sem("weights_in"), 16)
            act.sem_inc(passed, 1)
            act.wait_ge(sem("ones_row"), 1)
            act.sem_inc(passed, 1)
            act.wait_ge(sem("bn_ready"), 1)
            act.sem_inc(passed, 1)
            for b in range(B):
                act.wait_ge(sem("conv1"), b + 1)
                act.sem_inc(passed, 1)
                for k in range(8):
                    last = act.activation(YC[0:16, k * 512:(k + 1) * 512], PS[0:16, k, :], ACT.Relu,
                                          bias=bnv[:, 3:4], scale=bnv[:, 1:2])
                last.then_inc(sem("relu"), 1)
                act.wait_ge(sem("conv2"), b + 1)
                act.sem_inc(passed, 1)
                if b:
                    act.wait_ge(sem("dyn_out"), 16 * b)
                    act.sem_inc(passed, 1)
                for k in range(8):
                    last = act.activation(WD[:, k * 512:(k + 1) * 512], PS[0:9, k, :], ACT.Copy)
                last.then_inc(sem("dyn"), 1)
            barrier(act, 1)
            barrier(act, 2)

            def take_t(what, it, scale=None):
                act.wait_ge(sem(what + "_t"), it + 1)
                act.sem_inc(passed, 1)
                if scale is None:
                    act.activation(XT[0:C, :], PS[0:C, 0, 0:W3], ACT.Copy).then_inc(sem(what + "_ts"), 1)
                else:
                    act.activation(XT[0:C, :], PS[0:C, 0, 0:W3], ACT.Identity, scale=scale)\
                       .then_inc(sem(what + "_ts"), 1)

            def take_q(lay, what, it):
                act.wait_ge(sem(what + "_p"), it + 1)
                act.sem_inc(passed, 1)
                act.activation(QK[:, :, 0:lay.nq], PS[:, 1:1 + L, 0:lay.nq], ACT.Copy, scale=lay.qscale)
                n = lay.nq + lay.nk + lay.nv
                act.activation(QK[:, :, lay.nq:n], PS[:, 1:1 + L, lay.nq:n], ACT.Copy)\
                   .then_inc(s(lay, "q"), 1)

            barrier(act, BASE0 + 1)
            with act.Fori(0, B) as b:
                with act.Fori(0, NTRIO) as t:
                    it = b * NTRIO + t
                    take_t("a0", it)
                    take_q(ATT0, "a0", it)
                    put_turned(act, ATT0, it, t, 0)
                barrier(act, BASE0 + 2 + 3 * b)
                heads(act, ATT0, lambda kvh, rr: act_head(act, ATT0, b, kvh, rr))
                barrier(act, BASE0 + 3 + 3 * b)
                with act.Fori(0, NTRIO) as t:
                    it = b * NTRIO + t
                    act.wait_ge(sem("p0_t"), it + 1)
                    act.sem_inc(passed, 1)
                    act.activation(XT[0:C, :], PSH[0:C, 0:W3], ACT.Copy).then_inc(sem("p0_ts"), 1)
                barrier(act, BASE0 + 4 + 3 * b)
            barrier(act, BASE1 + 1)
            with act.Fori(0, B) as b:
                with act.Fori(0, NTRIO) as t:
                    it = b * NTRIO + t
                    take_t("a1", it, wt("ln1", C))
                    take_q(ATT1, "a1", it)
                    put_turned(act, ATT1, it, t, 0)
                barrier(act, BASE1 + 2 + 3 * b)
                heads(act, ATT1, lambda kvh, rr: act_head(act, ATT1, b, kvh, rr))
                barrier(act, BASE1 + 3 + 3 * b)
                with act.Fori(0, NTRIO) as t:
                    it = b * NTRIO + t
                    take_t("p1", it)
                    take_t("m", it, wt("ln2", C))
                    act.wait_ge(sem("m_logit"), it + 1)
                    act.sem_inc(passed, 1)
                    act.activation(S1[:, 1, 0:L * NE], S1[:, 0, 0:L * NE], ACT.Exp).then_inc(sem("m_exp"), 1)
                    for i in range(2 * NE):
                        act.wait_ge(sem("m_ab"), it * 16 + i + 1)
                        act.sem_inc(passed, 1)
                        act.wait_ge(sem("m_g"), it * 16 + i + 1)
                        act.sem_inc(passed, 1)
                        act.activation(E1[0:HH, 2 * (i % 3):2 * (i % 3) + 2, :].rearrange("p a b -> p (a b)"),
                                       PS[0:HH, 2 * (i % 3), 0:W3], ACT.Tanh, scale=0.5).then_inc(sem("m_s"), 1)
                barrier(act, BASE1 + 4 + 3 * b)
            barrier(act, BASE2 + 1)
            with act.Fori(0, B) as b:
                with act.Fori(0, NTRIO) as t:
                    it = b * NTRIO + t
                    take_t("a2", it)
                    act.wait_ge(sem("a2_c"), it + 1)
                    act.sem_inc(passed, 1)
                    act.activation(CT[:, :], PS[:, 1, 0:W3], ACT.Copy).then_inc(sem("a2c_ts"), 1)
                    take_q(ATT2, "a2c", it)
                    put_turned(act, ATT2, it, t, 0)
                barrier(act, BASE2 + 2 + 3 * b)
                heads(act, ATT2, lambda kvh, rr: act_head(act, ATT2, b, kvh, rr))
                barrier(act, BASE2 + 3 + 3 * b)
                barrier(act, BASE2 + 4 + 3 * b)
            barrier(act, BASE3 + 1)
            with act.Fori(0, B) as b:
                with act.Fori(0, NTRIO) as t:
                    it = b * NTRIO + t
                    take_t("sx", it)
            barrier(act, BASE3 + 2)
            with act.Fori(0, B) as b:
                with act.Fori(0, 4) as n:
                    with act.Fori(0, NTRIO) as t:
                        it = (b * 4 + n) * NTRIO + t
                        act.wait_ge(sem("a3_t"), it + 1)
                        act.sem_inc(passed, 1)
                        act.activation(XT[0:D, :], PS[0:D, 0, 0:W3], ACT.Copy).then_inc(sem("a3_ts"), 1)
                        take_q(ATT3, "a3", it)
                        put_turned(act, ATT3, it, t, 0)
                    barrier(act, BASE3 + 3 + MEET3 * b + 2 * n)
                    heads(act, ATT3, lambda kvh, rr: act_head(act, ATT3, b * 4 + n, kvh, rr))
                    barrier(act, BASE3 + 4 + MEET3 * b + 2 * n)
                with act.Fori(0, NTRIO) as t:
                    it = b * NTRIO + t
                    act.wait_ge(sem("p3_omt"), it + 1)
                    act.sem_inc(passed, 1)
                    act.activation(OT[:, :, :], PS[:, 0:2, 0:W3], ACT.Copy).then_inc(sem("p3_ot"), 1)
                    act.wait_ge(sem("p3_logit"), it * 2 + 1)
                    act.sem_inc(passed, 1)
                    act.activation(S1[:, 1, :], S1[:, 0, :], ACT.Exp).then_inc(sem("p3_exp"), 1)
                    for i in range(3):
                        take_t("p3", it * 3 + i)
                    act.wait_ge(sem("p3_logit"), it * 2 + 2)
                    act.sem_inc(passed, 1)
                    act.activation(S1[:, 1, 0:L * 4], S1[:, 0, 0:L * 4], ACT.Exp).then_inc(sem("p3_exp"), 1)
                barrier(act, BASE3 + 3 + MEET3 * b + 8)

        @block.vector
        def _(dve):
            dve.wait_ge(sem("weights_in"), 16)
            dve.sem_inc(passed, 1)
            at = COLS["bn"][0]
            b1, mean, gamma, var, beta = (WP[0:16, at + i:at + i + 1] for i in range(5))
            dve.wait_ge(sem("bn_rstd"), 1)
            dve.sem_inc(passed, 1)
            dve.tensor_tensor(bnv[:, 1:2], bnv[:, 2:3], gamma, ALU.mult)
            dve.tensor_tensor(bnv[:, 0:1], b1, mean, ALU.subtract)
            dve.drain()
            dve.tensor_tensor(bnv[:, 2:3], bnv[:, 0:1], bnv[:, 1:2], ALU.mult)
            dve.drain()
            dve.tensor_tensor(bnv[:, 3:4], bnv[:, 2:3], beta, ALU.add).then_inc(sem("bn_ready"), 1)
            for b in range(B):
                dve.wait_ge(sem("shift_in"), 16 * 24 * (b + 1))
                dve.sem_inc(passed, 1)
                dve.wait_ge(sem("rows_in"), 16 * 2 * (b + 1))
                dve.sem_inc(passed, 1)
                hb = H[:, b * NT:b * NT + 32, :]
                for k in range(9):
                    i, j = divmod(k, 3)
                    w = WB[:, k, :].unsqueeze(1).broadcast_to([P, 32, IMG])
                    dve.tensor_tensor(hb if k == 0 else TM[:, k % 2], XS[:, i, :, j:j + IMG], w, ALU.mult)
                    dve.drain()
                    if k:
                        dve.tensor_tensor(hb, hb, TM[:, k % 2], ALU.add)
                dve.drain()
                dve.sem_inc(sem("shift_free"), 1)
            barrier(dve, 1)
            dve.sem_inc(sem("maxbank_free"), L)
            dve.sem_inc(sem("exps"), L)
            dve.sem_inc(sem("values"), BUFS)
            dve.sem_inc(sem("out_free"), 1)
            dve.sem_inc(sem("rests_dve"), 1)
            dve.sem_inc(sem("rests_pool"), L + 1)
            for lay in (ATT0, ATT1, ATT3):
                dve.sem_inc(s(lay, "outs_put"), 1)
            dve.sem_inc(sem("p0_done"), 1)
            dve.sem_inc(sem("a3_stage_free"), 1)
            dve.sem_inc(sem("m_g"), 3)
            dve.sem_inc(sem("m_acc"), 2)
            dve.wait_ge(sem("text_in"), 16 * B)
            dve.sem_inc(passed, 1)
            barrier(dve, 2)

            def take_k(lay, it):
                dve.wait_ge(s(lay, "q"), it + 1)
                dve.sem_inc(passed, 1)

            barrier(dve, BASE0 + 1)
            with dve.Fori(0, B) as b:
                dve_layernorm(dve, b, "ln0", SX[:, 0:NT, :])
                with dve.Fori(0, NTRIO) as t:
                    it = b * NTRIO + t
                    dve.tensor_scalar(STG[:, :, :], XN[:, bass.ds(t * L, L), :], -10000.0, 10000.0, ALU.max, ALU.min)\
                       .then_inc(sem("a0_in"), 1)
                    take_k(ATT0, it)
                    dve_split(dve, ATT0, it)
                    put_turned(dve, ATT0, it, t, 1)
                    dve.wait_ge(s(ATT0, "put"), 2 * it + 2)
                    dve.sem_inc(passed, 1)
                    dve.sem_inc(passed, 1)
                barrier(dve, BASE0 + 2 + 3 * b)
                heads(dve, ATT0, lambda kvh, rr: dve_head(dve, ATT0, b, kvh, rr, kvh * ATT0.rep + rr))
                barrier(dve, BASE0 + 3 + 3 * b)
                with dve.Fori(0, NTRIO) as t:
                    it = b * NTRIO + t
                    dve.wait_ge(sem("p0_p"), it + 1)
                    dve.sem_inc(passed, 1)
                    hb = H[:, bass.ds(b * NT + t * L, L), :]
                    dve.tensor_tensor(hb, hb, PS[:, 1:1 + L, 0:C], ALU.add).then_inc(sem("p0_done"), 1)
                barrier(dve, BASE0 + 4 + 3 * b)

            def softmax(src, n, k, what, it):
                m = S1[:, 3, 0:n]
                lo = S1[:, 0, 0:n * k].rearrange("p (a b) -> p a b", b=k)
                ex = S1[:, 1, 0:n * k].rearrange("p (a b) -> p a b", b=k)
                pr = S1[:, 2, 0:n * k].rearrange("p (a b) -> p a b", b=k)
                dve.tensor_reduce(m, src, AX, ALU.max, negate=True)
                dve.drain()
                dve.tensor_tensor(lo, src, m.unsqueeze(2).broadcast_to([P, n, k]), ALU.add)\
                   .then_inc(sem(what + "_logit"), 1)
                dve.wait_ge(sem(what + "_exp"), it + 1)
                dve.sem_inc(passed, 1)
                dve.tensor_reduce(S1[:, 4, 0:n], ex, AX, ALU.add)
                dve.drain()
                dve.reciprocal(m, S1[:, 4, 0:n])
                dve.drain()
                dve.tensor_tensor(pr, ex, m.unsqueeze(2).broadcast_to([P, n, k]), ALU.mult)
                dve.drain()
                return pr

            def rms(dst, src, n, what, k):
                sq = SX[:, 0:n, :]
                dve.tensor_tensor(sq, src, src, ALU.mult)
                dve.drain()
                dve.tensor_reduce(st[:, 2, 0:n], sq, AX, ALU.add)
                dve.drain()
                dve.tensor_scalar(st[:, 3, 0:n], st[:, 2, 0:n], 1.0 / C, None, ALU.mult)
                ask_rstd(dve, what, k)
                return dve.tensor_tensor(dst, src, st[:, 2, 0:n].unsqueeze(2).broadcast_to([P, n, C]), ALU.mult)

            dve.wait_ge(sem("table_in"), 16)
            dve.sem_inc(passed, 1)
            for e in range(NE):
                dve.memset(before[:, e, :], 0.0)
                if e:
                    dve.drain()
                    dve.memset(before[:, e, 0:e], 1.0)
            barrier(dve, BASE1 + 1)
            with dve.Fori(0, B) as b:
                dve_layernorm(dve, b, "ln1", SX[:, 0:NT, :])
                sq = SX[:, 0:NT, :]
                xr_ = SX[:, NT:2 * NT, :]
                rms(xr_, XN[:, :, :], NT, "rms", b)
                dve.drain()
                with dve.Fori(0, NTRIO) as t:
                    it = b * NTRIO + t
                    dve.tensor_copy(STG[:, :, :], SX[:, bass.ds(t * L + NT, L), :]).then_inc(sem("a1_in"), 1)
                    n = ATT1.nq + ATT1.nk
                    nh = n // D
                    take_k(ATT1, it)
                    for l in range(L):
                        cos = RT[:, 0, bass.ds(t * L + l, 1), :].broadcast_to([P, nh, D])
                        sin = RT[:, 1, bass.ds(t * L + l, 1), :].broadcast_to([P, nh, D])
                        q = QK[:, l, 0:n].rearrange("p (h d) -> p h d", d=D)
                        r1 = R1[:, l, 0:n].rearrange("p (h d) -> p h d", d=D)
                        r2 = R2[:, l, 0:n].rearrange("p (h d) -> p h d", d=D)
                        dve.tensor_tensor(r1, q, cos, ALU.mult)
                        dve.tensor_tensor(r2[:, :, 0:D // 2], q[:, :, D // 2:D], sin[:, :, 0:D // 2], ALU.mult)
                        dve.tensor_tensor(r2[:, :, D // 2:D], q[:, :, 0:D // 2], sin[:, :, D // 2:D], ALU.mult)
                    dve.drain()
                    dve.tensor_tensor(QK[:, :, 0:n], R1[:, :, 0:n], R2[:, :, 0:n], ALU.add)
                    dve.drain()
                    dve_split(dve, ATT1, it)
                    put_turned(dve, ATT1, it, t, 1)
                    dve.wait_ge(s(ATT1, "put"), 2 * it + 2)
                    dve.sem_inc(passed, 1)
                    dve.sem_inc(passed, 1)
                barrier(dve, BASE1 + 2 + 3 * b)
                heads(dve, ATT1, lambda kvh, rr: dve_head(dve, ATT1, b, kvh, rr, kvh * ATT1.rep + rr))
                barrier(dve, BASE1 + 3 + 3 * b)
                with dve.Fori(0, NTRIO) as t:
                    it = b * NTRIO + t
                    dve.tensor_copy(STG[:, :, :], Y64[:, bass.ds(t * L, L), :]).then_inc(sem("p1_in"), 1)
                    dve.wait_ge(sem("p1_p"), it + 1)
                    dve.sem_inc(passed, 1)
                    dve.tensor_tensor(X1[:, :, :], XN[:, bass.ds(t * L, L), :], PS[:, 1:1 + L, 0:C], ALU.add)
                    dve.drain()
                    rms(OM[:, :, 0:C], X1[:, :, :], L, "rm1", it).then_inc(sem("m_in"), 1)
                    dve.wait_ge(sem("m_p"), it + 1)
                    dve.sem_inc(passed, 1)
                    pr = softmax(PS[:, 1:1 + L, 0:NE], L, NE, "m", it)
                    dve.sem_inc(sem("m_router_read"), 1)
                    gt = E1[:, 6, 64:128].rearrange("p (a b) -> p a b", b=NE)
                    eq = E1[:, 6, 128:192].rearrange("p (a b) -> p a b", b=NE)
                    rank = S1[:, 5, 0:L * NE].rearrange("p (a b) -> p a b", b=NE)
                    for l in range(L):
                        mine = pr[:, l, :].unsqueeze(2).broadcast_to([P, NE, NE])
                        other = pr[:, l, :].unsqueeze(1).broadcast_to([P, NE, NE])
                        dve.tensor_tensor(gt, other, mine, ALU.is_gt)
                        dve.tensor_tensor(eq, other, mine, ALU.is_equal)
                        dve.drain()
                        dve.tensor_tensor(eq, eq, before, ALU.mult)
                        dve.drain()
                        dve.tensor_tensor(gt, gt, eq, ALU.add)
                        dve.drain()
                        dve.tensor_reduce(rank[:, l, :], gt, AX, ALU.add)
                        dve.drain()
                    sel = S1[:, 6, 0:L * NE].rearrange("p (a b) -> p a b", b=NE)
                    dve.tensor_scalar(sel, rank, 1.5, None, ALU.is_lt)
                    dve.drain()
                    dve.tensor_tensor(rank, sel, pr, ALU.mult)
                    dve.drain()
                    dve.tensor_reduce(S1[:, 4, 0:L], rank, AX, ALU.add)
                    dve.drain()
                    dve.tensor_scalar(S1[:, 3, 0:L], S1[:, 4, 0:L], 1e-9, None, ALU.add)
                    dve.drain()
                    dve.reciprocal(S1[:, 4, 0:L], S1[:, 3, 0:L])
                    dve.drain()
                    dve.tensor_scalar(S1[:, 3, 0:L], S1[:, 4, 0:L], 0.5, None, ALU.mult)
                    dve.drain()
                    dve.tensor_tensor(sel, rank, S1[:, 3, 0:L].unsqueeze(2).broadcast_to([P, L, NE]), ALU.mult)
                    dve.drain()

                    def add_expert(f):
                        dve.wait_ge(sem("m_o"), it * NE + f + 1)
                        dve.sem_inc(passed, 1)
                        tmp = STG[:, :, :]
                        dve.tensor_tensor(tmp, PS[:, 6 + f % 2, 0:L * C].rearrange("p (l c) -> p l c", c=C),
                                          sel[:, :, f].unsqueeze(2).broadcast_to([P, L, C]), ALU.mult)\
                           .then_inc(sem("m_acc"), 1)
                        dve.drain()
                        dve.tensor_tensor(X1[:, :, :], X1[:, :, :], tmp, ALU.add)
                        dve.drain()

                    for i in range(2 * NE):
                        e, hf = divmod(i, 2)
                        dve.wait_ge(sem("m_s"), it * 16 + i + 1)
                        dve.sem_inc(passed, 1)
                        th = E1[0:HH, 2 * (i % 3):2 * (i % 3) + 2, :].rearrange("p a b -> p (a b)")
                        ra = (R1, R2)[i % 2][0:HH, :, :].rearrange("p a b -> p (a b)")[:, 0:W3]
                        dve.scalar_tensor_tensor(out=ra, in0=th, scalar=1.0,
                                                 in1=PS[0:HH, 2 * (i % 3), 0:W3], op0=ALU.add, op1=ALU.mult)
                        dve.drain()
                        dve.tensor_tensor(G[:, e % 2, hf, :], ra,
                                          PS[0:HH, 2 * (i % 3) + 1, 0:W3], ALU.mult).then_inc(sem("m_g"), 1)
                        if hf and e >= 1:
                            add_expert(e - 1)
                    add_expert(NE - 1)
                    hb = H[:, bass.ds(b * NT + t * L, L), :]
                    dve.tensor_tensor(hb, hb, X1[:, :, :], ALU.add)
                    dve.drain()
                barrier(dve, BASE1 + 4 + 3 * b)
            dve.wait_ge(sem("table_in"), 32)
            dve.sem_inc(passed, 1)
            barrier(dve, BASE2 + 1)
            with dve.Fori(0, B) as b:
                dve_layernorm(dve, b, "ln2", SX[:, 0:NT, :])
                with dve.Fori(0, NTRIO) as t:
                    it = b * NTRIO + t
                    dve.tensor_copy(STG[:, :, :], XN[:, bass.ds(t * L, L), :]).then_inc(sem("a2_in"), 1)
                    take_k(ATT2, it)
                    for half in range(2):
                        q = QK[:, :, half * C + 48:half * C + 64].rearrange("p l (i two) -> p l i two", two=2)
                        q1, q2 = q[:, :, :, 0], q[:, :, :, 1]
                        cos = RT[:, 0, bass.ds(t * L, L), 0:D // 2]
                        sin = RT[:, 1, bass.ds(t * L, L), 0:D // 2]
                        r = [R2[:, :, i * 8:(i + 1) * 8] for i in range(4)]
                        dve.tensor_tensor(r[0], q1, cos, ALU.mult)
                        dve.tensor_tensor(r[1], q2, sin, ALU.mult)
                        dve.tensor_tensor(r[2], q1, sin, ALU.mult)
                        dve.tensor_tensor(r[3], q2, cos, ALU.mult)
                        dve.drain()
                        dve.tensor_tensor(q1, r[0], r[1], ALU.subtract)
                        dve.tensor_tensor(q2, r[2], r[3], ALU.add)
                        dve.drain()
                    dve_split(dve, ATT2, it)
                    put_turned(dve, ATT2, it, t, 1)
                    dve.wait_ge(s(ATT2, "put"), 2 * it + 2)
                    dve.sem_inc(passed, 1)
                    dve.sem_inc(passed, 1)
                barrier(dve, BASE2 + 2 + 3 * b)
                heads(dve, ATT2, lambda kvh, rr: dve_head(dve, ATT2, b, kvh, rr, 0))
                barrier(dve, BASE2 + 3 + 3 * b)
                hb = H[:, bass.ds(b * NT, NT), :]
                dve.tensor_tensor(hb, hb, Y64[:, :, :], ALU.add)
                barrier(dve, BASE2 + 4 + 3 * b)
            barrier(dve, BASE3 + 1)
            with dve.Fori(0, B) as b:
                dve_layernorm(dve, b, "ln3", Y[:, :, 0:C])
                with dve.Fori(0, NTRIO) as t:
                    it = b * NTRIO + t
                    dve.tensor_copy(STG[:, :, :], XN[:, bass.ds(t * L, L), :]).then_inc(sem("sx_in"), 1)
                    dve.wait_ge(sem("sx_p"), it + 1)
                    dve.sem_inc(passed, 1)
                    dve.tensor_copy(SX[:, bass.ds(b * NT + t * L, L), :], PS[:, 1:1 + L, 0:C])
                    dve.drain()
            barrier(dve, BASE3 + 2)
            g4 = L * 4

            def norm16(dst, src, g, b_, k):
                mu, sq = S1[:, 3, 0:g4], E1[:, 7, 0:L * C].rearrange("p (a b) -> p a b", b=D)
                var, mean, rstd = S1[:, 4, 0:g4], st[:, 3, 0:g4], st[:, 2, 0:g4]
                xc = E1[:, 6, 0:L * C].rearrange("p (a b) -> p a b", b=D)
                dve.tensor_reduce(var, src, AX, ALU.add)
                dve.drain()
                dve.tensor_scalar(mu, var, 1.0 / D, None, ALU.mult)
                dve.drain()
                dve.tensor_tensor(xc, src, mu.unsqueeze(2).broadcast_to([P, g4, D]), ALU.subtract)
                dve.drain()
                dve.tensor_tensor(sq, xc, xc, ALU.mult)
                dve.drain()
                dve.tensor_reduce(var, sq, AX, ALU.add)
                dve.drain()
                dve.tensor_scalar(mean, var, 1.0 / D, None, ALU.mult)
                ask_rstd(dve, "n16", k)
                dve.tensor_tensor(sq, xc, rstd.unsqueeze(2).broadcast_to([P, g4, D]), ALU.mult)
                dve.drain()
                dve.tensor_tensor(xc, sq, wt(g, P).unsqueeze(1).broadcast_to([P, g4, D]), ALU.mult)
                dve.drain()
                return dve.tensor_tensor(dst, xc, wt(b_, P).unsqueeze(1).broadcast_to([P, g4, D]), ALU.add)

            def by16(ap):
                return ap.rearrange("p l (n d) -> p (l n) d", d=D)

            with dve.Fori(0, B) as b:
                with dve.Fori(0, 4) as n:
                    with dve.Fori(0, NTRIO) as t:
                        it = (b * 4 + n) * NTRIO + t
                        take_k(ATT3, it)
                        dve_split(dve, ATT3, it)
                        put_turned(dve, ATT3, it, t, 1)
                        dve.wait_ge(s(ATT3, "put"), 2 * it + 2)
                        dve.sem_inc(passed, 1)
                        dve.sem_inc(sem("a3_stage_free"), 1)
                    barrier(dve, BASE3 + 3 + MEET3 * b + 2 * n)
                    heads(dve, ATT3, lambda kvh, rr: dve_head(dve, ATT3, b * 4 + n, kvh, rr, n * 4 + rr))
                    barrier(dve, BASE3 + 4 + MEET3 * b + 2 * n)
                with dve.Fori(0, NTRIO) as t:
                    it = b * NTRIO + t
                    nz = E1[:, 0, :].rearrange("p (l c) -> p l c", c=C)
                    dve.tensor_scalar(nz, SX[:, bass.ds(b * NT + t * L, L), :], 0.0, None, ALU.not_equal)
                    dve.drain()
                    for l in range(L):
                        dve.tensor_tensor(OM[:, l, :].rearrange("p (n e d) -> p n e d", e=4, d=D),
                                          Y[:, bass.ds(t * L + l, 1), :].rearrange("p a (n e d) -> p (a n) e d", e=4, d=D),
                                          nz[:, l, :].rearrange("p (n d) -> p n d", d=D).unsqueeze(2)
                                          .broadcast_to([P, 4, 4, D]), ALU.mult)
                    dve.drain()
                    dve.sem_inc(sem("p3_om"), 1)
                    dve.wait_ge(sem("p3_gate"), it + 1)
                    dve.sem_inc(passed, 1)
                    gl = E1[:, 1, 0:L * 16].rearrange("p (l c) -> p l c", c=16)
                    dve.tensor_tensor(gl, PS[:, 2, 0:L * 16].rearrange("p (l c) -> p l c", c=16),
                                      wt("gateb", P).unsqueeze(1).broadcast_to([P, L, 16]), ALU.add)
                    dve.drain()
                    gs = softmax(gl.rearrange("p l (n e) -> p (l n) e", e=4), g4, 4, "p3", it * 2)
                    for l in range(L):
                        om = OM[:, l, :].rearrange("p (n e d) -> p n e d", e=4, d=D)
                        dve.tensor_tensor(om, om, gs[:, 4 * l:4 * l + 4, :].unsqueeze(3).broadcast_to([P, 4, 4, D]),
                                          ALU.mult)
                    dve.drain()
                    m4 = OM[:, :, :].rearrange("p l (n e d) -> p (l n) (e d)", e=4, d=D)
                    half = E1[:, 2:4, :].rearrange("p a b -> p (a b)")[:, 0:g4 * 32].rearrange("p (a b) -> p a b", b=32)
                    dve.tensor_tensor(half, m4[:, :, 0:32], m4[:, :, 32:64], ALU.add)
                    dve.drain()
                    mix = by16(E1[:, 4, :].rearrange("p (l c) -> p l c", c=C))
                    dve.tensor_tensor(mix, half[:, :, 0:D], half[:, :, D:2 * D], ALU.add)
                    dve.drain()
                    mx = E1[:, 4, :].rearrange("p (l c) -> p l c", c=C)
                    dve.tensor_tensor(mx[:, :, 0:D], mx[:, :, 0:D], SX[:, bass.ds(t * L, L), 0:D], ALU.add)
                    dve.tensor_tensor(mx[:, :, D:C], mx[:, :, D:C], SX[:, bass.ds(t * L + NT, L), D:C], ALU.add)
                    dve.drain()
                    fx = X1[:, :, :]
                    norm16(by16(fx), mix, "lng", "lnb", it * 2)
                    dve.drain()
                    dve.tensor_scalar(nz, fx, 0.0, None, ALU.not_equal)
                    dve.tensor_copy(STG[:, :, :], fx).then_inc(sem("p3_in"), 1)
                    dve.wait_ge(sem("p3_p"), it * 3 + 1)
                    dve.sem_inc(passed, 1)
                    dve.scalar_tensor_tensor(out=STG[:, :, :], in0=PS[:, 1:1 + L, 0:C], scalar=0.0, in1=nz,
                                             op0=ALU.max, op1=ALU.mult).then_inc(sem("p3_in"), 1)
                    dve.wait_ge(sem("p3_p"), it * 3 + 2)
                    dve.sem_inc(passed, 1)
                    dve.tensor_tensor(mx, PS[:, 1:1 + L, 0:C], nz, ALU.mult)
                    dve.drain()
                    dve.tensor_tensor(nz, mx, fx, ALU.add)
                    dve.drain()
                    fo = E1[:, 5, :].rearrange("p (l c) -> p l c", c=C)
                    norm16(by16(fo), by16(nz), "fng", "fnb", it * 2 + 1)
                    dve.drain()
                    dve.tensor_copy(STG[:, :, :], fo).then_inc(sem("p3_in"), 1)
                    dve.wait_ge(sem("p3_p"), it * 3 + 3)
                    dve.sem_inc(passed, 1)
                    fg = softmax(PS[:, 1:1 + L, 0:4], L, 4, "p3", it * 2 + 1)
                    dve.tensor_tensor(by16(mx), by16(fo), fg.rearrange("p a b -> p (a b)").unsqueeze(2)
                                      .broadcast_to([P, g4, D]), ALU.mult)
                    dve.drain()
                    hb = H[:, bass.ds(b * NT + t * L, L), :]
                    dve.tensor_tensor(hb, hb, mx, ALU.add)
                    dve.drain()
                barrier(dve, BASE3 + 3 + MEET3 * b + 8)
            dve.sem_inc(sem("final"), 1)


def kernel(**inputs):
    import numpy as np
    import concourse.bacc as bacc
    from concourse import mybir as mb
    from concourse.bass_utils import run_bass_kernel_spmd as run

    a = {k: np.ascontiguousarray(v) for k, v in inputs.items()}
    wp = np.zeros((P, NCOLS), np.float32)

    def put(name, block, col=0, row=0):
        at = COLS[name][0] + col
        wp[row:row + block.shape[0], at:at + block.shape[1]] = block

    put("conv1", a["L0_tok_conv1_w"].T)
    for i, name in enumerate(("conv1_b", "bn_mean", "bn_gamma", "bn_var", "bn_beta")):
        put("bn", a["L0_tok_" + name][:, None], i)
    put("conv2", a["L0_tok_conv2_w"].T)
    put("conv2", a["L0_tok_conv2_b"][None, :], 0, 16)
    for i, name in enumerate("qkv"):
        put("wqkv0", a["L0_attn_W" + name].T, 64 * i)
        put("wqkv0", a["L0_attn_b" + name][None, :], 64 * i, 64)
    put("wo0", a["L0_attn_Wo"].T)
    put("wo0", a["L0_attn_bo"][None, :], 0, 64)
    put("ln1", a["L0_ffn_ln1_w"][:, None])
    put("ln2", a["L0_ffn_ln2_w"][:, None])
    put("wqkv1", a["L0_ffn_wq"].T, 0)
    put("wqkv1", a["L0_ffn_wk"].T, 64)
    put("wqkv1", a["L0_ffn_wv"].T, 96)
    put("wo1", a["L0_ffn_wo"].T)
    put("router", a["L0_ffn_router_w"].T)
    for e in range(NE):
        put("w1", a["L0_ffn_w1"][e].T, e * HID)
        put("w3", a["L0_ffn_w3"][e].T, e * HID)
        for hf in range(2):
            put("w2", a["L0_ffn_w2"][e].T[hf * HH:(hf + 1) * HH], (hf * NE + e) * C)
    put("wcomp", a["L1_attn_Wq_comp"], 0)
    put("wcomp", a["L1_attn_Wkv_comp"], 64)
    put("wsec", a["L1_attn_Wqc"], 0)
    put("wsec", a["L1_attn_Wqr"], 48)
    put("wsec", a["L1_attn_Wkc"], 64, 64)
    put("wsec", a["L1_attn_Wkr"], 112, 64)
    put("wsec", a["L1_attn_Wv"], 128, 64)
    put("hl", a["L1_ffn_hl_w"].reshape(64, 64).T)
    put("hl", a["L1_ffn_hl_b"].reshape(1, 64), 0, 64)
    for n in range(4):
        for e in range(4):
            put("wn", a["L1_ffn_wq"][n, e].T, n * 96 + e * D)
        put("wn", a["L1_ffn_wk"][n].T, n * 96 + 64)
        put("wn", a["L1_ffn_wv"][n].T, n * 96 + 80)
        put("gate", a["L1_ffn_gate_w"][n].T, n * 4, (n % 2) * 64)
        for name in ("fc1", "fc2"):
            put(name, a[f"L1_ffn_{name}_w"].T, n * D, n * D)
            put(name, a[f"L1_ffn_{name}_b"][None, :], n * D, 64)
    put("gateb", np.tile(a["L1_ffn_gate_b"].reshape(1, 16), (P, 1)))
    for col, name in (("lng", "ln_g"), ("lnb", "ln_b"), ("fng", "fnorm_g"), ("fnb", "fnorm_b")):
        put(col, np.tile(a["L1_ffn_" + name][None, :], (P, 1)))
    put("fgate", a["L1_ffn_fgate_w"].T)

    inv = 1.0 / 10000.0 ** (np.arange(0, D, 2, dtype=np.float32) / D)
    ang = np.outer(np.arange(T, dtype=np.float32), inv)
    cos = np.cos(np.concatenate([ang, ang], -1)).astype(np.float32)
    sin = np.sin(np.concatenate([ang, ang], -1)).astype(np.float32)
    sin[:, :D // 2] = -sin[:, :D // 2]
    by_tile = lambda m: np.ascontiguousarray(m.reshape(NT, P, -1).transpose(1, 0, 2))
    rope0 = np.stack([by_tile(cos), by_tile(sin)], 1).astype(np.float32)
    theta = (np.float32(1.0) / np.float32(10000.0) ** (np.arange(D // 2, dtype=np.float32) / np.float32(D // 2)))
    ang = (np.arange(T, dtype=np.float32)[:, None] * theta[None, :]).astype(np.float32)
    rope1 = np.stack([by_tile(np.cos(ang)), by_tile(np.sin(ang))], 1).astype(np.float32)

    nc = bacc.Bacc("TRN2", target_bir_lowering=False, num_devices=1)
    arrays = {"x_dram": a["x"], "txt_dram": a["txt"], "wpack_dram": wp, "rope0_dram": rope0, "rope1_dram": rope1}
    aps = [nc.dram_tensor(k, v.shape, mb.dt.from_np(v.dtype), kind="ExternalInput").ap() for k, v in arrays.items()]
    wd = nc.dram_tensor("wd_scratch", (B, 9, IMG * IMG), mb.dt.float32, kind="Internal").ap()
    out = nc.dram_tensor("out_dram", (B, T, C), mb.dt.float32, kind="ExternalOutput").ap()
    build(nc, *aps, wd, out)
    r = run(nc, [arrays], core_ids=[0])
    return r.results[0]["out_dram"]
```
